# Optimizing a Trainium2 kernel written in Bass

```python
import numpy as np
import jax
import jax.numpy as jnp

def _softmax(x, axis=-1):
    return jax.nn.softmax(x, axis=axis)

def _gelu(x):
    return jax.nn.gelu(x, approximate=True)

def _silu(x):
    return jax.nn.silu(x)

def _sigmoid(x):
    return jax.nn.sigmoid(x)

def _layernorm(x, axis=-1, eps=1e-05):
    m = jnp.mean(x, axis=axis, keepdims=True)
    v = jnp.var(x, axis=axis, keepdims=True)
    return (x - m) / jnp.sqrt(v + eps)

def _scatter_add(tgt, idx, src, axis=0):
    return tgt.at[idx].add(src)

def _segment_sum(src, seg, n):
    return jax.ops.segment_sum(src, seg, n)
kernel_name = 'mk_flamingo_gated_d1_seqx_r2_fa9369'

def setup_inputs(seed: int=0):
    np.random.seed(seed)
    _w = jnp.asarray

    def _rec_inputs():
        import jax
        import jax.numpy as jnp
        _rk = jax.random.key(seed)
        x = 7.22e-05 + 1 * jax.random.normal(jax.random.fold_in(_rk, 1), (8, 512, 1024), jnp.float32)
        _lenS = 512 - jax.random.randint(jax.random.fold_in(_rk, 7), (8,), 0, max(1, 512 // 4) + 1, jnp.int32)
        _lenS2 = 512 - jax.random.randint(jax.random.fold_in(_rk, 8), (8,), 0, max(1, 512 // 4) + 1, jnp.int32)
        _ctx_2048P = jax.random.normal(jax.random.fold_in(_rk, 11), (8, 16, 1024), jnp.float32)
        _ctx_2048c = jax.random.dirichlet(jax.random.fold_in(_rk, 511), 0.3 * jnp.ones((16,), jnp.float32), (8, 512))
        _ctx_2048t = jnp.einsum('bsk,bkd->bsd', _ctx_2048c, _ctx_2048P)
        _ctx_2048t = _ctx_2048t * jax.lax.rsqrt(jnp.mean(jnp.square(_ctx_2048t)) + 1e-12) * 0.953939
        ctx_2048 = 4.13588e-05 + 0.999923 * (_ctx_2048t + 0.3 * jax.random.normal(jax.random.fold_in(_rk, 611), (8, 512, 1024), jnp.float32))
        _validS = jnp.arange(512)[None, :] < _lenS[:, None]
        _validS2 = jnp.arange(512)[None, :] < _lenS2[:, None]
        _causal = jnp.tril(jnp.ones((512, 512), dtype=bool))
        mask_SxS2_bc0 = jnp.logical_not(jnp.broadcast_to(_validS2[0:1, :], (512, 512)))
        mask_BxS2_bk0 = jnp.logical_not(jnp.broadcast_to(_validS2[:, :], (8, 512)))
        _g = jax.random.normal(jax.random.fold_in(_rk, 9001), (2, 1), jnp.float32)
        _g = jnp.sign(_g) * jnp.maximum(jnp.abs(_g), 1.0) + (_g == 0) * 1.0
        g_xattn = _g[0]
        g_ffn = _g[1]
        return (x, ctx_2048, mask_SxS2_bc0, mask_BxS2_bk0, g_xattn, g_ffn)
    x, ctx_2048, mask_SxS2_bc0, mask_BxS2_bk0, g_xattn, g_ffn = _rec_inputs()

    def _L0_xattn_setup():
        import jax, jax.numpy as jnp
        import numpy as np
        B, LQ, LKV = (4, 512, 512)
        HID, H, G = (1024, 32, 8)
        HD = HID // H
        HPG = H // G
        key = jax.random.key(seed)
        ks = jax.random.split(key, 10)
        s = 0.02
        inp = {'X': jax.random.normal(ks[0], (B, LQ, HID), jnp.float32), 'encoder_output': jax.random.normal(ks[1], (B, LKV, HID), jnp.float32), 'causal_mask': jnp.triu(jnp.ones((LQ, LKV), bool), 1), 'padding_mask': jnp.zeros((B, LKV), bool).at[B // 2:, LKV - LKV // 4:].set(True), 'Wq': jax.random.normal(ks[2], (HID, HID), jnp.float32) * s, 'bq': jnp.zeros((HID,), jnp.float32), 'Wk': jax.random.normal(ks[3], (G * HD, HID), jnp.float32) * s, 'bk': jnp.zeros((G * HD,), jnp.float32), 'Wv': jax.random.normal(ks[4], (G * HD, HID), jnp.float32) * s, 'bv': jnp.zeros((G * HD,), jnp.float32), 'Wo': jax.random.normal(ks[5], (HID, HID), jnp.float32) * s, 'bo': jnp.zeros((HID,), jnp.float32)}
        return inp
    _L0_xattn_all = _L0_xattn_setup()
    _L0_xattn_in = {k: v for k, v in _L0_xattn_all.items() if k in ('Wq', 'bq', 'Wk', 'bk', 'Wv', 'bv', 'Wo', 'bo')}
    del _L0_xattn_all

    def _L0_ffn_setup():
        import jax, jax.numpy as jnp
        import numpy as np
        from jax import lax
        H = 1024
        I = 512
        E = 32
        K = 4
        SH_I = 1024
        EPS = 1e-06

        def _rmsnorm(x, w, eps=EPS):
            var = jnp.mean(jnp.square(x.astype(jnp.float32)), axis=-1, keepdims=True)
            return (x * lax.rsqrt(var + eps)).astype(x.dtype) * w
        key = jax.random.key(seed)
        ks = jax.random.split(key, 8)
        s = lambda d: 1.0 / np.sqrt(d)
        return {'x': jax.random.normal(ks[0], (2, 1024, H), jnp.float32), 'norm_w': jnp.ones((H,), jnp.float32), 'router_w': jax.random.normal(ks[1], (E, H), jnp.float32) * s(H), 'w1': jax.random.normal(ks[2], (E, H, 2 * I), jnp.float32) * s(H), 'w2': jax.random.normal(ks[3], (E, I, H), jnp.float32) * s(I), 'sg': jax.random.normal(ks[4], (H, SH_I), jnp.float32) * s(H), 'su': jax.random.normal(ks[5], (H, SH_I), jnp.float32) * s(H), 'sd': jax.random.normal(ks[6], (SH_I, H), jnp.float32) * s(SH_I)}
    _L0_ffn_all = _L0_ffn_setup()
    _L0_ffn_in = {k: v for k, v in _L0_ffn_all.items() if k in ('norm_w', 'router_w', 'w1', 'w2', 'sg', 'su', 'sd')}
    del _L0_ffn_all
    return {'x': x, 'ctx_2048': ctx_2048, 'mask_SxS2_bc0': mask_SxS2_bc0, 'mask_BxS2_bk0': mask_BxS2_bk0, 'g_xattn': g_xattn, 'g_ffn': g_ffn, 'L0_xattn_Wq': _L0_xattn_in['Wq'], 'L0_xattn_bq': _L0_xattn_in['bq'], 'L0_xattn_Wk': _L0_xattn_in['Wk'], 'L0_xattn_bk': _L0_xattn_in['bk'], 'L0_xattn_Wv': _L0_xattn_in['Wv'], 'L0_xattn_bv': _L0_xattn_in['bv'], 'L0_xattn_Wo': _L0_xattn_in['Wo'], 'L0_xattn_bo': _L0_xattn_in['bo'], 'L0_ffn_norm_w': _L0_ffn_in['norm_w'], 'L0_ffn_router_w': _L0_ffn_in['router_w'], 'L0_ffn_w1': _L0_ffn_in['w1'], 'L0_ffn_w2': _L0_ffn_in['w2'], 'L0_ffn_sg': _L0_ffn_in['sg'], 'L0_ffn_su': _L0_ffn_in['su'], 'L0_ffn_sd': _L0_ffn_in['sd']}

def reference(x, ctx_2048, mask_SxS2_bc0, mask_BxS2_bk0, g_xattn, g_ffn, L0_xattn_Wq, L0_xattn_bq, L0_xattn_Wk, L0_xattn_bk, L0_xattn_Wv, L0_xattn_bv, L0_xattn_Wo, L0_xattn_bo, L0_ffn_norm_w, L0_ffn_router_w, L0_ffn_w1, L0_ffn_w2, L0_ffn_sg, L0_ffn_su, L0_ffn_sd):
    import jax
    import jax.numpy as jnp

    def _L0_xattn_ref(X, encoder_output, causal_mask, padding_mask, Wq, bq, Wk, bk, Wv, bv, Wo, bo):
        import jax, jax.numpy as jnp
        import numpy as np
        B, LQ, LKV = (4, 512, 512)
        HID, H, G = (1024, 32, 8)
        HD = HID // H
        HPG = H // G
        b = X.shape[0]
        q = X @ Wq.T + bq
        k = encoder_output @ Wk.T + bk
        v = encoder_output @ Wv.T + bv
        q = q.reshape(b, LQ, G, HPG, HD).transpose(0, 2, 3, 1, 4)
        k = k.reshape(b, LKV, G, HD).transpose(0, 2, 1, 3)
        v = v.reshape(b, LKV, G, HD).transpose(0, 2, 1, 3)
        scores = jnp.einsum('bgrqd,bgkd->bgrqk', q, k) / jnp.sqrt(jnp.float32(HD))
        scores = jnp.where(causal_mask[None, None, None, :, :], -jnp.inf, scores)
        scores = jnp.where(padding_mask[:, None, None, None, :], -jnp.inf, scores)
        w = jax.nn.softmax(scores, axis=-1)
        out = jnp.einsum('bgrqk,bgkd->bgrqd', w, v)
        out = out.reshape(b, H, LQ, HD).transpose(0, 2, 1, 3).reshape(b, LQ, HID)
        return out @ Wo.T + bo

    def _L0_ffn_ref(x, norm_w, router_w, w1, w2, sg, su, sd):
        import jax, jax.numpy as jnp
        import numpy as np
        from jax import lax
        H = 1024
        I = 512
        E = 32
        K = 4
        SH_I = 1024
        EPS = 1e-06

        def _rmsnorm(x, w, eps=EPS):
            var = jnp.mean(jnp.square(x.astype(jnp.float32)), axis=-1, keepdims=True)
            return (x * lax.rsqrt(var + eps)).astype(x.dtype) * w
        B, S, _ = x.shape
        residual = x
        h = _rmsnorm(x, norm_w)
        flat = h.reshape(-1, H)
        T = flat.shape[0]
        logits = flat.astype(jnp.float32) @ router_w.T
        scores = jax.nn.softmax(logits, axis=-1)
        topk_w, topk_ids = lax.top_k(scores, K)
        topk_w = topk_w / jnp.sum(topk_w, axis=-1, keepdims=True)
        ids = topk_ids.reshape(-1)
        sort_idx = jnp.argsort(ids)
        tok_idx = sort_idx // K
        xs = jnp.take(flat, tok_idx, axis=0)
        group_sizes = jnp.bincount(ids, length=E).astype(jnp.int32)
        gu = lax.ragged_dot(xs, w1, group_sizes)
        g, u = jnp.split(gu, 2, axis=-1)
        act = jax.nn.silu(g) * u
        ys = lax.ragged_dot(act, w2, group_sizes)
        y = jnp.zeros((T * K, H), ys.dtype).at[sort_idx].set(ys)
        routed = jnp.sum(y.reshape(T, K, H) * topk_w[..., None].astype(ys.dtype), axis=1)
        shared = jax.nn.silu(flat @ sg) * (flat @ su) @ sd
        out = residual + (routed + shared).reshape(B, S, H)
        return out
    x = x + jnp.tanh(g_xattn[0]) * _L0_xattn_ref(_layernorm(x, axis=-1), ctx_2048, mask_SxS2_bc0, mask_BxS2_bk0, L0_xattn_Wq, L0_xattn_bq, L0_xattn_Wk, L0_xattn_bk, L0_xattn_Wv, L0_xattn_bv, L0_xattn_Wo, L0_xattn_bo)
    x = x + jnp.tanh(g_ffn[0]) * _L0_ffn_ref(_layernorm(x, axis=-1), L0_ffn_norm_w, L0_ffn_router_w, L0_ffn_w1, L0_ffn_w2, L0_ffn_sg, L0_ffn_su, L0_ffn_sd)
    return x

_drawn_inputs = setup_inputs


def setup_inputs(seed=0):
    import zlib

    import numpy as np

    out = dict(_drawn_inputs(seed))
    spreads = {'L0_xattn_bq': (0.0, 0.331),
     'L0_xattn_bk': (0.0, 0.8),
     'L0_xattn_bv': (0.0, 0.1),
     'L0_xattn_bo': (0.0, 0.1),
     'L0_ffn_norm_w': (1.0, 0.2)}
    factors = {}
    for name, (base, spread) in spreads.items():
        noise = np.random.default_rng([zlib.crc32(name.encode()), seed]).standard_normal(out[name].shape)
        drawn = base * np.exp(spread * noise) if base else spread * noise
        out[name] = jnp.asarray(drawn.astype(out[name].dtype))
    for name, factor in factors.items():
        out[name] = (out[name] * factor).astype(out[name].dtype)
    return out
```

```python
from contextlib import ExitStack

import concourse.bass as bass
from concourse import mybir

F32 = mybir.dt.float32
F32R = mybir.dt.float32r
BF16 = mybir.dt.bfloat16
I32 = mybir.dt.int32
U32 = mybir.dt.uint32
U8 = mybir.dt.uint8
ACT = mybir.ActivationFunctionType
ALU = mybir.AluOpType
AX = mybir.AxisListType

P = 128
BATCH, SEQ, DM = 8, 512, 1024
TOKENS = BATCH * SEQ
HEADS, GROUPS = 32, 8
HPG = HEADS // GROUPS
HD = DM // HEADS
KV = GROUPS * HD
NEXP, TOPK, FF = 32, 4, 512
KC = DM // P
FC = FF // P
ST = SEQ // P
TT = TOKENS // P
SEGMENTS = NEXP + 2
MAX_TILES = TOKENS * TOPK // P + 2 * NEXP
MASKED = -1.0e30
LN_EPS, RMS_EPS = 1e-5, 1e-6
SCALE = HD ** -0.5


class Tools:

    def __init__(self, nc, ctx, stage):
        self.nc, self.ctx, self.stage = nc, ctx, stage

    def sb(self, name, shape, dt):
        return self.ctx.enter_context(self.nc.sbuf_tensor(f"{self.stage}_{name}", shape, dt))

    def ps(self, name, shape, dt=F32):
        return self.ctx.enter_context(self.nc.psum_tensor(f"{self.stage}_{name}", shape, dt))

    def sem(self, name):
        return self.ctx.enter_context(self.nc.semaphore(f"{self.stage}_{name}"))

    def sems(self, name, n):
        return [self.sem(f"{name}{i}") for i in range(n)]


def carry(eng, ticks):
    eng.sem_inc(ticks, 1)


def after(eng, sem, count):
    if not (isinstance(count, int) and count <= 0):
        eng.wait_ge(sem, count)


def in_pairs(eng, n, body):
    body(0, 0, 0, False)
    body(1, 0, 1, False)
    with eng.Fori(1, n // 2 - 1) as j:
        body(j * 2, j, 0, False)
        body(j * 2 + 1, j, 1, False)
    body(n - 2, n // 2 - 1, 0, False)
    body(n - 1, n // 2 - 1, 1, True)


def in_fours(eng, n, body):
    for slot in range(4):
        body(slot, 0, slot)
    with eng.Fori(1, n // 4 - 1) as j:
        for slot in range(4):
            body(j * 4 + slot, j, slot)
    for slot in range(4):
        body(n - 4 + slot, n // 4 - 1, slot)


def within(i, n):
    return not isinstance(i, int) or 0 <= i < n


def three_passes(nc, out, a, b, first, last):
    nc.tensor.matmul(out, a[0], b[0], start=first, stop=False)
    nc.tensor.matmul(out, a[1], b[0], start=False, stop=False)
    return nc.tensor.matmul(out, a[0], b[1], start=False, stop=last)


def make_identity(nc, pool, ident, done):
    nc.gpsimd.memset(ident[:, :], 0.0).then_inc(done, 1)
    pool.wait_ge(done, 1)
    nc.gpsimd.affine_select(out=ident[:, :], in_=ident[:, :], compare_op=ALU.not_equal, fill=1.0,
                            base=0, pattern=[[-1, P]], channel_multiplier=1).then_inc(done, 1)


def low_part(nc, out, x, hi):
    return nc.vector.tensor_tensor(out, x, hi.bitcast(F32), ALU.subtract)


def project_queries(nc, x, wq_t, bq_col, q_parts):
    with ExitStack() as ctx:
        t = Tools(nc, ctx, "q")
        ticks = t.sem("ticks")
        ident = t.sb("ident", [P, P], F32)
        w = [t.sb("w_hi", [P, KC, DM], F32R), t.sb("w_lo", [P, KC, DM], F32R)]
        w_raw = t.sb("w_raw", [P, 2, DM], F32)
        xt = [[t.sb(f"xt_hi{s}", [P, KC, SEQ], F32R), t.sb(f"xt_lo{s}", [P, KC, SEQ], F32R)] for s in range(2)]
        x_in = t.sb("x_in", [P, 2, DM], F32)
        xn = t.sb("xn", [P, 2, DM], F32)
        stats = t.sb("stats", [P, 2, 6], F32)
        mean_var = t.sb("mean_var", [P, 2], F32)
        var_eps = t.sb("var_eps", [P, 1], F32)
        std = t.sb("std", [P, 1], F32)
        rstd = t.sb("rstd", [P, 1], F32)
        bq = t.sb("bq", [P, KC], F32)
        q_out = t.sb("q_out", [P, 2, 2, SEQ], F32R)
        tp = [t.ps(f"tp{s}", [P, KC, P]) for s in range(2)]
        acc = [t.ps(f"acc{s}", [P, SEQ]) for s in range(2)]

        s_id, s_bq = t.sem("ident"), t.sem("bq")
        w_in, w_hi, w_lo = t.sems("w_in", 2), t.sem("w_hi"), t.sem("w_lo")
        x_loaded, xn_ready = t.sems("x_loaded", 2), t.sem("xn_ready")
        ln_step, s_var, s_std = t.sem("ln_step"), t.sem("var"), t.sem("std")
        tp_ready, tp_hi, tp_lo = t.sem("tp_ready"), t.sem("tp_hi"), t.sem("tp_lo")
        q_ready, q_hi, q_lo = t.sem("q_ready"), t.sem("q_hi"), t.sem("q_lo")
        q_stored = t.sems("q_stored", 2)
        xv = x.rearrange("(n p) d -> n p d", p=P)
        wv = wq_t.rearrange("(c p) f -> c p f", p=P)
        qv = q_parts.rearrange("(n p) h t -> n p h t", p=P)

        with nc.Block() as block:
            @block.sync
            def _(sp):
                sp.dma_start(bq[:, :], bq_col).then_inc(s_bq, 16)
                for n in range(2):
                    sp.dma_start(x_in[:, n, :], xv[n]).then_inc(x_loaded[n], 16)
                for c in range(KC):
                    after(sp, w_lo, c - 1)
                    sp.dma_start(w_raw[:, c % 2, :], wv[c]).then_inc(w_in[c % 2], 16)
                with sp.Fori(1, TT // 2) as j:
                    for s in range(2):
                        sp.wait_ge(xn_ready, j * 2 + (s - 1))
                        carry(sp, ticks)
                        sp.dma_start(x_in[:, s, :], xv[j * 2 + s]).then_inc(x_loaded[s], 16)

            @block.gpsimd
            def _(pool):
                make_identity(nc, pool, ident, s_id)
                with pool.Fori(0, BATCH) as b:
                    for m in range(KC):
                        pool.wait_ge(q_lo, b * KC + (m + 1))
                        pool.dma_start(qv[b * KC + m], q_out[:, m % 2, :, :].bitcast(F32)).then_inc(q_stored[m % 2], 16)
                for s in range(2):
                    pool.wait_ge(q_stored[s], 16 * BATCH * KC // 2)

            @block.scalar
            def _(act):
                def root(n):
                    act.wait_ge(s_var, n + 1)
                    nc.scalar.activation(std[:, :], var_eps[:, :], ACT.Sqrt).then_inc(s_std, 1)

                def high_of_transposed(n, tile, slot):
                    act.wait_ge(tp_ready, n + 1)
                    nc.scalar.copy(xt[slot][0][:, :, tile * P:(tile + 1) * P], tp[tile % 2][:, :, :])\
                        .then_inc(tp_hi, 1)

                root(0)
                for c in range(KC):
                    act.wait_ge(w_in[c % 2], 16 * (c // 2 + 1))
                    nc.scalar.copy(w[0][:, c, :], w_raw[:, c % 2, :]).then_inc(w_hi, 1)
                for n in range(1, ST + 1):
                    root(n)
                    high_of_transposed(n - 1, n - 1, 0)
                act.wait_ge(s_bq, 16)

                def step(i, half, slot, last):
                    for k in range(ST):
                        if not last:
                            high_of_transposed(i * ST + (ST + k), k, 1 - slot)
                            if not (isinstance(i, int) and i * ST + ST + k + 1 >= TT):
                                root(i * ST + (ST + k + 1))
                        for m in (2 * k, 2 * k + 1):
                            act.wait_ge(q_ready, i * KC + (m + 1))
                            after(act, q_stored[m % 2], (i * (KC // 2) + m // 2) * 16)
                            nc.scalar.activation(q_out[:, m % 2, 0, :], acc[m % 2][:, :], ACT.Identity,
                                                 bias=bq[:, m:m + 1]).then_inc(q_hi, 1)
                in_pairs(act, BATCH, step)

            @block.vector
            def _(dve):
                def norm(n, half, slot):
                    dve.wait_ge(x_loaded[slot], half * 16 + 16)
                    after(dve, xn_ready, n)
                    nc.vector.bn_stats(stats[:, 0, :], x_in[:, slot, 0:DM // 2])
                    nc.vector.bn_stats(stats[:, 1, :], x_in[:, slot, DM // 2:DM]).then_inc(ln_step, 1)
                    dve.wait_ge(ln_step, n * 3 + 1)
                    carry(dve, ticks)
                    nc.vector.bn_aggr(mean_var[:, :], stats[:, :, :]).then_inc(ln_step, 1)
                    dve.wait_ge(ln_step, n * 3 + 2)
                    nc.vector.tensor_scalar(var_eps[:, :], mean_var[:, 1:2], LN_EPS, None, ALU.add)\
                        .then_inc(s_var, 1)
                    dve.wait_ge(s_std, n + 1)
                    nc.vector.reciprocal(rstd[:, :], std[:, :]).then_inc(ln_step, 1)
                    dve.wait_ge(ln_step, n * 3 + 3)
                    after(dve, tp_ready, n - 1)
                    nc.vector.tensor_scalar(xn[:, slot, :], x_in[:, slot, :], mean_var[:, 0:1], rstd[:, :],
                                            ALU.subtract, ALU.mult).then_inc(xn_ready, 1)

                def low_of_transposed(n, tile, slot):
                    dve.wait_ge(tp_hi, n + 1)
                    cols = slice(tile * P, (tile + 1) * P)
                    low_part(nc, xt[slot][1][:, :, cols], tp[tile % 2][:, :, :], xt[slot][0][:, :, cols])\
                        .then_inc(tp_lo, 1)

                norm(0, 0, 0)
                for c in range(KC):
                    dve.wait_ge(w_hi, c + 1)
                    low_part(nc, w[1][:, c, :], w_raw[:, c % 2, :], w[0][:, c, :]).then_inc(w_lo, 1)
                for n in range(1, ST + 1):
                    norm(n, n // 2, n % 2)
                    low_of_transposed(n - 1, n - 1, 0)
                dve.wait_ge(s_bq, 16)

                def step(i, half, slot, last):
                    for k in range(ST):
                        if not last:
                            low_of_transposed(i * ST + (ST + k), k, 1 - slot)
                            if not (isinstance(i, int) and i * ST + ST + k + 1 >= TT):
                                norm(i * ST + (ST + k + 1), i * (ST // 2) + (ST + k + 1) // 2, (k + 1) % 2)
                        for m in (2 * k, 2 * k + 1):
                            dve.wait_ge(q_hi, i * KC + (m + 1))
                            nc.vector.scalar_tensor_tensor(q_out[:, m % 2, 1, :], acc[m % 2][:, :], bq[:, m:m + 1],
                                                           q_out[:, m % 2, 0, :].bitcast(F32), ALU.add,
                                                           ALU.subtract).then_inc(q_lo, 1)
                in_pairs(dve, BATCH, step)

            @block.tensor
            def _(pe):
                pe.wait_ge(s_id, 2)

                def transpose_tile(n, tile):
                    pe.wait_ge(xn_ready, n + 1)
                    after(pe, tp_lo, n - 1)
                    for c in range(KC):
                        done = nc.tensor.transpose(tp[tile % 2][:, c, :], xn[:, tile % 2, c * P:(c + 1) * P],
                                                   ident[:, :])
                    done.then_inc(tp_ready, 1)

                for n in range(ST):
                    transpose_tile(n, n)
                pe.wait_ge(w_lo, KC)

                def step(i, half, slot, last):
                    for k in range(ST):
                        if not last:
                            transpose_tile(i * ST + (ST + k), k)
                        if k == 0:
                            pe.wait_ge(tp_lo, i * ST + ST)
                        for m in (2 * k, 2 * k + 1):
                            after(pe, q_lo, i * KC + (m - 1))
                            for c in range(KC):
                                done = three_passes(nc, acc[m % 2][:, :],
                                                    [part[:, c, m * P:(m + 1) * P] for part in w],
                                                    [part[:, c, :] for part in xt[slot]], c == 0, c == KC - 1)
                            done.then_inc(q_ready, 1)
                in_pairs(pe, BATCH, step)


def project_keys(nc, ctx_t, wk_t, wv_t, bk_col, bv_row, k_parts, v_rows):
    with ExitStack() as ctx:
        t = Tools(nc, ctx, "k")
        ticks = t.sem("ticks")
        wk = [t.sb("wk_hi", [P, KC, KV], F32R), t.sb("wk_lo", [P, KC, KV], F32R)]
        wv = [t.sb("wv_hi", [P, KC, KV], F32R), t.sb("wv_lo", [P, KC, KV], F32R)]
        w_raw = t.sb("w_raw", [P, 2, KC, KV], F32)
        c_in = [t.sb(f"c_in{s}", [P, KC, SEQ], F32) for s in range(2)]
        ct = [[t.sb(f"ct_hi{s}", [P, KC, SEQ], F32R), t.sb(f"ct_lo{s}", [P, KC, SEQ], F32R)] for s in range(2)]
        bk = t.sb("bk", [P, KV // P], F32)
        bv = t.sb("bv", [P, KV], F32)
        k_out = t.sb("k_out", [P, 2, 2, SEQ], F32R)
        v_out = t.sb("v_out", [P, 2, KV], F32)
        k_acc = [t.ps(f"k_acc{s}", [P, SEQ]) for s in range(2)]
        v_acc = [t.ps(f"v_acc{s}", [P, KV]) for s in range(2)]
        s_bias, w_in, w_hi, w_lo = t.sem("bias"), t.sem("w_in"), t.sem("w_hi"), t.sem("w_lo")
        c_loaded, c_hi, c_lo = t.sems("c_loaded", 2), t.sem("c_hi"), t.sem("c_lo")
        k_ready, k_hi, k_lo = t.sem("k_ready"), t.sem("k_hi"), t.sem("k_lo")
        v_ready, v_copied = t.sem("v_ready"), t.sem("v_copied")
        k_stored, v_stored = t.sems("k_stored", 2), t.sems("v_stored", 2)
        kv = k_parts.rearrange("(n p) h t -> n p h t", p=P)
        MK = KV // P
        cv = ctx_t.rearrange("b (c p) t -> b p c t", p=P)
        vv = v_rows.rearrange("b g (k p) d -> b k p g d", p=P)

        with nc.Block() as block:
            @block.sync
            def _(sp):
                sp.dma_start(w_raw[:, 0, :, :], wk_t.rearrange("(c p) f -> p c f", p=P)).then_inc(w_in, 16)
                sp.dma_start(w_raw[:, 1, :, :], wv_t.rearrange("(c p) f -> p c f", p=P)).then_inc(w_in, 16)
                sp.dma_start(bk[:, :], bk_col).then_inc(s_bias, 16)
                sp.dma_start(bv[:, :], bv_row.partition_broadcast(P)).then_inc(s_bias, 16)
                for s in range(2):
                    sp.dma_start(c_in[s][:, :, :], cv[s]).then_inc(c_loaded[s], 16)
                with sp.Fori(1, BATCH // 2) as j:
                    for s in range(2):
                        sp.wait_ge(c_lo, j * 2 + (s - 1))
                        carry(sp, ticks)
                        sp.dma_start(c_in[s][:, :, :], cv[j * 2 + s]).then_inc(c_loaded[s], 16)

            @block.gpsimd
            def _(pool):
                with pool.Fori(0, BATCH) as b:
                    for m in range(MK):
                        pool.wait_ge(k_lo, b * MK + (m + 1))
                        pool.dma_start(kv[b * MK + m], k_out[:, m, :, :].bitcast(F32)).then_inc(k_stored[m], 16)
                    for k in range(ST):
                        pool.wait_ge(v_copied, b * ST + (k + 1))
                        pool.dma_start(vv[b, k], v_out[:, k % 2, :].rearrange("p (g d) -> p g d", g=GROUPS))\
                            .then_inc(v_stored[k % 2], 16)
                for m in range(MK):
                    pool.wait_ge(k_stored[m], 16 * BATCH)
                for s in range(2):
                    pool.wait_ge(v_stored[s], 16 * BATCH * ST // 2)

            @block.scalar
            def _(act):
                act.wait_ge(w_in, 32)
                nc.scalar.copy(wk[0][:, :, :], w_raw[:, 0, :, :]).then_inc(w_hi, 1)
                nc.scalar.copy(wv[0][:, :, :], w_raw[:, 1, :, :]).then_inc(w_hi, 1)

                def high_of_context(i, half, slot):
                    act.wait_ge(c_loaded[slot], half * 16 + 16)
                    after(act, v_ready, i * ST - ST)
                    nc.scalar.copy(ct[slot][0][:, :, :], c_in[slot][:, :, :]).then_inc(c_hi, 1)

                high_of_context(0, 0, 0)
                act.wait_ge(s_bias, 32)

                def step(i, half, slot, last):
                    if not last:
                        high_of_context(i + 1, half + slot, 1 - slot)
                    for m in range(MK):
                        act.wait_ge(k_ready, i * MK + (m + 1))
                        after(act, k_stored[m], i * 16)
                        nc.scalar.activation(k_out[:, m, 0, :], k_acc[m][:, :], ACT.Identity,
                                             bias=bk[:, m:m + 1]).then_inc(k_hi, 1)
                in_pairs(act, BATCH, step)

            @block.vector
            def _(dve):
                for n, w in enumerate((wk, wv)):
                    dve.wait_ge(w_hi, n + 1)
                    low_part(nc, w[1][:, :, :], w_raw[:, n, :, :], w[0][:, :, :]).then_inc(w_lo, 1)

                def low_of_context(i, half, slot):
                    dve.wait_ge(c_hi, i + 1)
                    low_part(nc, ct[slot][1][:, :, :], c_in[slot][:, :, :], ct[slot][0][:, :, :]).then_inc(c_lo, 1)

                low_of_context(0, 0, 0)
                dve.wait_ge(s_bias, 32)

                def step(i, half, slot, last):
                    if not last:
                        low_of_context(i + 1, half + slot, 1 - slot)
                    for m in range(MK):
                        dve.wait_ge(k_hi, i * MK + (m + 1))
                        nc.vector.scalar_tensor_tensor(k_out[:, m, 1, :], k_acc[m][:, :], bk[:, m:m + 1],
                                                       k_out[:, m, 0, :].bitcast(F32), ALU.add,
                                                       ALU.subtract).then_inc(k_lo, 1)
                    for k in range(ST):
                        dve.wait_ge(v_ready, i * ST + (k + 1))
                        after(dve, v_stored[k % 2], (i * (ST // 2) + k // 2) * 16)
                        nc.vector.tensor_tensor(v_out[:, k % 2, :], v_acc[k % 2][:, :], bv[:, :], ALU.add)\
                            .then_inc(v_copied, 1)
                in_pairs(dve, BATCH, step)

            @block.tensor
            def _(pe):
                pe.wait_ge(w_lo, 2)

                def step(i, half, slot, last):
                    pe.wait_ge(c_lo, i + 1)
                    for m in range(MK):
                        after(pe, k_lo, i * MK + (m + 1 - MK))
                        for c in range(KC):
                            done = three_passes(nc, k_acc[m][:, :], [part[:, c, m * P:(m + 1) * P] for part in wk],
                                                [part[:, c, :] for part in ct[slot]], c == 0, c == KC - 1)
                        done.then_inc(k_ready, 1)
                    for k in range(ST):
                        after(pe, v_copied, i * ST + (k - 1))
                        for c in range(KC):
                            done = three_passes(nc, v_acc[k % 2][:, :],
                                                [part[:, c, k * P:(k + 1) * P] for part in ct[slot]],
                                                [part[:, c, :] for part in wv], c == 0, c == KC - 1)
                        done.then_inc(v_ready, 1)
                in_pairs(pe, BATCH, step)


def attention(nc, q_parts, k_parts, v_rows, mask_s, mask_st, mask_b, mask_b_col, o_cols):
    with ExitStack() as ctx:
        t = Tools(nc, ctx, "a")
        ticks = t.sem("ticks")
        STEPS = BATCH * GROUPS
        SLOTS4 = 4
        NQ = HPG * ST
        GR = 2 * ST
        D3, ROWS = 3 * HD, 3 * HD + 2
        ident = t.sb("ident", [P, P], F32)
        ident_bf = t.sb("ident_bf", [P, P], BF16)
        qs = [t.sb(f"qs{s}", [ROWS, HPG, SEQ], F32R) for s in range(SLOTS4)]
        ks = [t.sb(f"ks{s}", [ROWS, SEQ], F32R) for s in range(SLOTS4)]
        vs = [t.sb(f"vs{s}", [P, ST, HD], F32) for s in range(SLOTS4)]
        ones = t.sb("ones", [P, HD], F32)
        ms_raw = t.sb("ms_raw", [P, ST, SEQ], U8)
        mst_raw = t.sb("mst_raw", [P, ST, SEQ], U8)
        ms = t.sb("ms", [P, ST, SEQ], BF16)
        mst = t.sb("mst", [P, ST, SEQ], BF16)
        mb_raw = t.sb("mb_raw", [P, SLOTS4, SEQ], U8)
        mb = t.sb("mb", [P, SLOTS4, SEQ], BF16)
        bias = [t.sb(f"bias{s}", [P, ST, SEQ], BF16) for s in range(2)]
        mbc_raw = t.sb("mbc_raw", [P, SLOTS4, ST], U8)
        mbc = t.sb("mbc", [P, SLOTS4, ST], F32)
        junk = t.sb("junk", [P, 2, SEQ], BF16)
        mx = t.sb("mx", [P, 2, NQ], F32)
        mt = t.sb("mt", [NQ, 2, 2, P], F32R)
        pt = t.sb("pt", [P, ST, HPG, SEQ], F32)
        pv_sb = t.sb("pv_sb", [P, SEQ], F32)
        rsum = t.sb("rsum", [P, SEQ], F32)
        o_out = t.sb("o_out", [P, 2, SEQ], F32)
        s1 = [t.ps(f"s1_{s}", [P, SEQ]) for s in range(2)]
        s2 = [t.ps(f"s2_{s}", [P, 2, SEQ]) for s in range(2)]
        pv = t.ps("pv", [P, SEQ])
        total = t.ps("total", [P, SEQ])
        mtp = s1[0][0:NQ, 0:P]
        s_id, s_mask, s_addend = t.sem("ident"), t.sem("mask"), t.sem("addend")
        s_ones = t.sem("ones")
        q_in, k_in, v_in = t.sems("q_in", SLOTS4), t.sems("k_in", SLOTS4), t.sems("v_in", SLOTS4)
        mb_in = t.sems("mb_in", SLOTS4)
        mb_wide, bias_ready = t.sem("mb_wide"), t.sem("bias_ready")
        s1_ready, s1_max = t.sem("s1_ready"), t.sem("s1_max")
        mt_ready, mt_hi, mt_lo, m_in = t.sem("mt_ready"), t.sem("mt_hi"), t.sem("mt_lo"), t.sems("m_in", SLOTS4)
        s2_ready, s_exp = t.sem("s2_ready"), t.sem("exp")
        pv_ready, pv_copied, total_inv, pv_out = (t.sem(n) for n in ("pv_ready", "pv_copied", "total_inv", "pv_out"))
        o_stored = t.sems("o_stored", 2)
        qv = q_parts.rearrange("(n r d) h t -> n h d r t", r=HPG, d=HD)
        kv = k_parts.rearrange("(n d) h t -> n h d t", d=HD)
        vv = v_rows.rearrange("b g (k p) d -> (b g) p k d", p=P)
        ov = o_cols.rearrange("(n p) t -> n p t", p=P)

        def ahead(quarter, slot, steps):
            return quarter + (slot + steps) // SLOTS4, (slot + steps) % SLOTS4

        with nc.Block() as block:
            @block.sync
            def _(sp):
                sp.dma_start(ms_raw[:, :, :], mask_s.rearrange("(k p) t -> p k t", p=P)).then_inc(s_mask, 16)
                sp.dma_start(mst_raw[:, :, :], mask_st.rearrange("(k p) t -> p k t", p=P)).then_inc(s_mask, 16)

                def load_mask(i, slot):
                    after(sp, mb_wide, i - (SLOTS4 - 1))
                    carry(sp, ticks)
                    sp.dma_start(mb_raw[:, slot, :], mask_b[i].partition_broadcast(P)).then_inc(mb_in[slot], 16)
                    sp.dma_start(mbc_raw[:, slot, :], mask_b_col[i]).then_inc(mb_in[slot], 16)

                def load(i, slot):
                    after(sp, s2_ready, (i - (SLOTS4 - 1)) * GR)
                    carry(sp, ticks)
                    for c, part in enumerate((0, 0, 1)):
                        sp.dma_start(qs[slot][c * HD:(c + 1) * HD, :, :].bitcast(F32), qv[i, part]).then_inc(q_in[slot], 16)
                    for c, part in enumerate((0, 1, 0)):
                        sp.dma_start(ks[slot][c * HD:(c + 1) * HD, :].bitcast(F32), kv[i, part]).then_inc(k_in[slot], 16)

                def load_values(i, slot):
                    after(sp, pv_ready, (i - (SLOTS4 - 1)) * ST)
                    carry(sp, ticks)
                    sp.dma_start(vs[slot][:, :, :], vv[i]).then_inc(v_in[slot], 16)

                def rows_of_maxima(i, slot):
                    sp.wait_ge(mt_lo, i + 1)
                    for part in range(2):
                        sp.dma_start(qs[slot][D3 + part:D3 + part + 1, :, :].bitcast(F32)
                                     .rearrange("o r (k p) -> o (r k) p", p=P),
                                     mt[:, slot % 2, part, :].bitcast(F32)).then_inc(m_in[slot], 16)

                for i in range(SLOTS4 - 1):
                    load_mask(i, i)
                    load(i, i)
                    load_values(i, i)
                rows_of_maxima(0, 0)

                def step(i, quarter, slot):
                    if within(i + 3, STEPS):
                        load_mask(i + 3, (slot + 3) % SLOTS4)
                        load(i + 3, (slot + 3) % SLOTS4)
                    if within(i + 1, STEPS):
                        rows_of_maxima(i + 1, (slot + 1) % SLOTS4)
                    if within(i + 3, STEPS):
                        load_values(i + 3, (slot + 3) % SLOTS4)
                in_fours(sp, STEPS, step)

            @block.gpsimd
            def _(pool):
                make_identity(nc, pool, ident, s_id)
                pool.wait_ge(s_id, 2)
                nc.gpsimd.tensor_copy(ident_bf[:, :], ident[:, :]).then_inc(s_id, 1)
                pool.wait_ge(s_mask, 32)
                nc.gpsimd.tensor_scalar(ms[:, :, :], ms_raw[:, :, :], MASKED, None, ALU.mult).then_inc(s_addend, 1)
                nc.gpsimd.tensor_scalar(mst[:, :, :], mst_raw[:, :, :], MASKED, None, ALU.mult).then_inc(s_addend, 1)
                pool.wait_ge(s_addend, 2)

                def addends(i, quarter, slot):
                    pool.wait_ge(mb_in[slot], quarter * 32 + 32)
                    after(pool, s_exp, (i - (SLOTS4 - 1)) * GR)
                    carry(pool, ticks)
                    nc.gpsimd.tensor_scalar(mb[:, slot, :], mb_raw[:, slot, :], MASKED, None, ALU.mult)
                    nc.gpsimd.tensor_scalar(mbc[:, slot, :], mbc_raw[:, slot, :], MASKED, None, ALU.mult)\
                        .then_inc(mb_wide, 1)
                    pool.wait_ge(mb_wide, i + 1)
                    after(pool, s1_max, (i - 1) * NQ)
                    for k in range(ST):
                        done = nc.gpsimd.tensor_tensor(bias[slot % 2][:, k, :], ms[:, k, :], mb[:, slot, :], ALU.add)
                    done.then_inc(bias_ready, 1)

                for i in range(SLOTS4 - 1):
                    addends(i, 0, i)

                def step(i, quarter, slot):
                    if within(i + 3, STEPS):
                        addends(i + 3, *ahead(quarter, slot, 3))
                in_fours(pool, STEPS, step)

            @block.scalar
            def _(act):
                def store(i, parity):
                    act.wait_ge(pv_out, i + 1)
                    carry(act, ticks)
                    act.dma_start(ov[i], o_out[:, parity, :]).then_inc(o_stored[parity], 16)

                def high_of_maxima(i, parity):
                    act.wait_ge(mt_ready, i + 1)
                    nc.scalar.mul(mt[:, parity, 0, :], mtp, -1.0).then_inc(mt_hi, 1)

                def free_banks(i):
                    act.wait_ge(pv_ready, i * ST + ST)
                    after(act, pv_out, i)
                    carry(act, ticks)
                    nc.scalar.copy(pv_sb[:, :], pv[:, :])
                    nc.scalar.copy(rsum[:, :], total[:, :]).then_inc(pv_copied, 1)

                high_of_maxima(0, 0)

                def step(i, quarter, slot):
                    for g in range(GR):
                        kt = g // 2
                        if g % 2 == 0:
                            after(act, pv_ready, i * ST + (kt + 1 - ST))
                        act.wait_ge(s2_ready, i * GR + (g + 1))
                        for v in range(2):
                            done = nc.scalar.activation(pt[:, kt, 2 * (g % 2) + v, :], s2[g % 2][:, v, :], ACT.Exp,
                                                        bias=mbc[:, slot, kt:kt + 1], scale=SCALE)
                        done.then_inc(s_exp, 1)
                        if g == 0 and within(i + 1, STEPS):
                            high_of_maxima(i + 1, (slot + 1) % 2)
                        if g == 1 and within(i - 1, STEPS):
                            free_banks(i - 1)
                        if g == GR - 1 and within(i - 1, STEPS):
                            store(i - 1, (slot + 1) % 2)
                    if not within(i + 1, STEPS):
                        free_banks(i)
                        store(i, slot % 2)
                in_fours(act, STEPS, step)
                for s in range(2):
                    act.wait_ge(o_stored[s], 16 * STEPS // 2)

            @block.vector
            def _(dve):
                def maxima(i, slot, n):
                    dve.wait_ge(s1_ready, i * NQ + (n + 1))
                    after(dve, s1_max, i * NQ + (n - 1))
                    carry(dve, ticks)
                    nc.vector.tensor_tensor_reduce(out=junk[:, n % 2, :], in0=s1[n % 2][:, :],
                                                   in1=bias[slot % 2][:, n % ST, :], scale=1.0, scalar=-3.0e38,
                                                   op0=ALU.add, op1=ALU.max,
                                                   accum_out=mx[:, slot % 2, n:n + 1]).then_inc(s1_max, 1)

                def low_of_maxima(i, parity):
                    dve.wait_ge(mt_hi, i + 1)
                    nc.vector.scalar_tensor_tensor(mt[:, parity, 1, :], mtp, -1.0,
                                                   mt[:, parity, 0, :].bitcast(F32), ALU.mult, ALU.subtract)\
                        .then_inc(mt_lo, 1)

                def invert(i, part):
                    if part == 0:
                        dve.wait_ge(pv_copied, i + 1)
                    cols = slice(part * P, (part + 1) * P)
                    nc.vector.reciprocal(rsum[:, cols], rsum[:, cols]).then_inc(total_inv, 1)

                def normalise(i, quarter, slot):
                    dve.wait_ge(total_inv, i * ST + ST)
                    after(dve, o_stored[slot % 2], quarter * 32 + (slot // 2) * 16)
                    carry(dve, ticks)
                    nc.vector.tensor_tensor(o_out[:, slot % 2, :], pv_sb[:, :], rsum[:, :], ALU.mult).then_inc(pv_out, 1)

                for s in range(SLOTS4):
                    nc.vector.memset(ks[s][D3:ROWS, :].bitcast(F32), 1.0).then_inc(s_ones, 1)
                nc.vector.memset(ones[:, :], 1.0).then_inc(s_ones, 1)
                for i in range(2):
                    dve.wait_ge(bias_ready, i + 1)
                    for n in range(NQ):
                        maxima(i, i, n)
                    if i == 0:
                        low_of_maxima(0, 0)

                def step(i, quarter, slot):
                    if within(i + 2, STEPS):
                        dve.wait_ge(bias_ready, i + 3)
                    if within(i + 1, STEPS):
                        low_of_maxima(i + 1, (slot + 1) % 2)
                    for n in range(NQ):
                        if n in (4, 6, 8, 10) and within(i - 1, STEPS):
                            invert(i - 1, (n - 4) // 2)
                        if n == 12 and within(i - 1, STEPS):
                            normalise(i - 1, *ahead(quarter, slot, -1))
                        if within(i + 2, STEPS):
                            maxima(i + 2, (slot + 2) % SLOTS4, n)
                    if not within(i + 1, STEPS):
                        for part in range(ST):
                            invert(i, part)
                        normalise(i, quarter, slot)
                in_fours(dve, STEPS, step)

            @block.tensor
            def _(pe):
                def scores_of_queries(i, slot, n):
                    after(pe, s1_max, i * NQ + (n - 1))
                    if n == 0:
                        after(pe, mt_lo, i)
                    qt = n % ST
                    nc.tensor.matmul(s1[n % 2][:, :], qs[slot][0:D3, n // ST, qt * P:(qt + 1) * P], ks[slot][0:D3, :],
                                     start=True, stop=True).then_inc(s1_ready, 1)

                def operands(quarter, slot):
                    pe.wait_ge(q_in[slot], quarter * 48 + 48)
                    pe.wait_ge(k_in[slot], quarter * 48 + 48)

                def transpose_maxima(i, parity):
                    pe.wait_ge(s1_max, i * NQ + NQ)
                    nc.tensor.transpose(mtp, mx[:, parity, :], ident[:, :]).then_inc(mt_ready, 1)

                def scores_of_keys(i, slot, g):
                    after(pe, s_exp, i * GR + (g - 1))
                    kt = g // 2
                    for v in range(2):
                        nc.tensor.matmul(s2[g % 2][:, v, :], ks[slot][:, kt * P:(kt + 1) * P],
                                         qs[slot][:, 2 * (g % 2) + v, :], start=True, stop=False)
                        done = nc.tensor.matmul(s2[g % 2][:, v, :], ident_bf[:, :], mst[:, kt, :], start=False,
                                                stop=True)
                    done.then_inc(s2_ready, 1)

                def column_tiles(out, weights, kt):
                    for r in range(HPG):
                        done = nc.tensor.matmul(out[r * HD:(r + 1) * HD, :], weights, pt[:, kt, r, :],
                                                start=kt == 0, stop=kt == ST - 1, tile_position=(0, r * HD))
                    return done

                def values(i, quarter, slot, kt):
                    pe.wait_ge(s_exp, i * GR + (2 * kt + 2))
                    if kt == 0:
                        pe.wait_ge(v_in[slot], quarter * 16 + 16)
                        after(pe, pv_copied, i)
                    column_tiles(pv, vs[slot][:, kt, :], kt)

                def sums(kt):
                    column_tiles(total, ones[:, :], kt).then_inc(pv_ready, 1)

                pe.wait_ge(s_id, 3)
                pe.wait_ge(s_ones, SLOTS4 + 1)
                pe.wait_ge(s_addend, 2)
                operands(0, 0)
                for n in range(NQ):
                    scores_of_queries(0, 0, n)
                transpose_maxima(0, 0)
                operands(0, 1)
                for n in range(NQ):
                    scores_of_queries(1, 1, n)

                def step(i, quarter, slot):
                    pe.wait_ge(m_in[slot], quarter * 32 + 32)
                    later = within(i + 2, STEPS)
                    if later:
                        operands(*ahead(quarter, slot, 2))
                    queries = iter(range(NQ if later else 0))

                    def some_queries(count):
                        for _ in range(count):
                            n = next(queries, None)
                            if n is not None:
                                scores_of_queries(i + 2, (slot + 2) % SLOTS4, n)

                    for kt in range(ST):
                        scores_of_keys(i, slot, 2 * kt)
                        if kt == 0 and within(i + 1, STEPS):
                            transpose_maxima(i + 1, (slot + 1) % 2)
                        some_queries(1 if kt else 0)
                        scores_of_keys(i, slot, 2 * kt + 1)
                        some_queries(1 if kt else 0)
                        before = (i, quarter, slot, kt - 1) if kt else (i - 1, *ahead(quarter, slot, -1), ST - 1)
                        if within(before[0], STEPS):
                            values(*before)
                            some_queries(1)
                            sums(before[3])
                        else:
                            some_queries(1)
                        some_queries(2 if kt else 1)
                    if not within(i + 1, STEPS):
                        values(i, quarter, slot, ST - 1)
                        sums(ST - 1)
                in_fours(pe, STEPS, step)


class Kept:

    def __init__(self, nc, ctx):
        t = Tools(nc, ctx, "kept")
        self.slots = t.sb("slots", [P, TT, TOPK], I32)
        self.entries = t.sb("entries", [P, TT, TOPK], I32)
        self.weights = t.sb("weights", [P, TT, TOPK], F32)
        self.expert = t.sb("expert", [P, TT, TOPK], F32)
        self.bounds = t.sb("bounds", [1, NEXP + 1], I32)
        self.gate = t.sb("gate", [P, 2], F32)


def close_attention(nc, x, o_cols, wo_t, bo, norm_w, router_t, gates, h_rows, base_rows, kept):
    with ExitStack() as ctx:
        t = Tools(nc, ctx, "c")
        ticks = t.sem("ticks")
        ident = t.sb("ident", [P, P], F32)
        w = [t.sb("w_hi", [P, KC, DM], F32R), t.sb("w_lo", [P, KC, DM], F32R)]
        rt = [t.sb("rt_hi", [P, KC, NEXP], F32R), t.sb("rt_lo", [P, KC, NEXP], F32R)]
        w_raw = t.sb("w_raw", [P, 2, DM], F32)
        rt_raw = t.sb("rt_raw", [P, KC, NEXP], F32)
        o_in = t.sb("o_in", [P, 2, KC, P], F32)
        x_in = t.sb("x_in", [P, 2, DM], F32)
        bo_wide = t.sb("bo_wide", [P, DM], F32)
        nw_wide = t.sb("nw_wide", [P, DM], F32)
        xb = t.sb("xb", [P, DM], F32)
        ot = [t.sb("ot_hi", [P, 2, KC, P], F32R), t.sb("ot_lo", [P, 2, KC, P], F32R)]
        ht = [t.sb("ht_hi", [P, KC, P], F32R), t.sb("ht_lo", [P, KC, P], F32R)]
        x1 = t.sb("x1", [P, DM], F32)
        z = t.sb("z", [P, DM], F32)
        zsq = t.sb("zsq", [P, DM], BF16)
        h = t.sb("h", [P, 2, DM], F32)
        base = t.sb("base", [P, 2, DM], F32)
        gated_z = t.sb("gated_z", [P, DM], F32)
        stats = t.sb("stats", [P, 2, 6], F32)
        mean_var = t.sb("mean_var", [P, 2], F32)
        small = t.sb("small", [P, 8], F32)
        logits = t.sb("logits", [P, NEXP], F32)
        top = t.sb("top", [P, 8], F32)
        top_i = t.sb("top_i", [P, 8], U32)
        ex = t.sb("ex", [P, TOPK], F32)
        tp = t.ps("tp", [P, KC, P])
        acc = t.ps("acc", [P, DM])
        lg = t.ps("lg", [P, NEXP])
        xv = x.rearrange("(n p) d -> n p d", p=P)
        ov = o_cols.rearrange("(b c p) (k t) -> b k p c t", c=KC, p=P, t=P)
        hv = h_rows.rearrange("(n p) d -> n p d", p=P)
        bv = base_rows.rearrange("(n p) d -> n p d", p=P)
        s_id, s_wide, s_gate, s_gbo = t.sem("ident"), t.sem("wide"), t.sem("gate"), t.sem("gbo")
        w_in, w_hi, w_lo = t.sems("w_in", 2), t.sem("w_hi"), t.sem("w_lo")
        r_in = t.sem("r_in")
        o_loaded, x_loaded = t.sems("o_loaded", 2), t.sems("x_loaded", 2)
        xb_ready = t.sem("xb_ready")
        ot_hi, ot_lo = t.sem("ot_hi"), t.sem("ot_lo")
        acc_ready, x1_ready = t.sem("acc_ready"), t.sem("x1_ready")
        ln_step, s_var, s_std, z_ready = t.sem("ln_step"), t.sem("var"), t.sem("std"), t.sem("z_ready")
        sq_ready, s_ms, s_rms, h_ready = t.sem("sq_ready"), t.sem("ms"), t.sem("rms"), t.sem("h_ready")
        gz_ready, base_ready = t.sem("gz_ready"), t.sem("base_ready")
        ht_ready, ht_hi, ht_lo = t.sem("ht_ready"), t.sem("ht_hi"), t.sem("ht_lo")
        lg_ready, lg_step, s_ex, w_step = t.sem("lg_ready"), t.sem("lg_step"), t.sem("ex"), t.sem("w_step")
        h_stored, base_stored = t.sems("h_stored", 2), t.sems("base_stored", 2)

        with nc.Block() as block:
            @block.sync
            def _(sp):
                sp.dma_start(kept.gate[:, 0:1], gates[0].partition_broadcast(P)).then_inc(s_wide, 16)
                sp.dma_start(kept.gate[:, 1:2], gates[1].partition_broadcast(P)).then_inc(s_wide, 16)
                sp.dma_start(bo_wide[:, :], bo.partition_broadcast(P)).then_inc(s_wide, 16)
                sp.dma_start(nw_wide[:, :], norm_w.partition_broadcast(P)).then_inc(s_wide, 16)
                sp.dma_start(rt_raw[:, :, :], router_t.rearrange("(c p) e -> p c e", p=P)).then_inc(r_in, 16)
                for c in range(KC):
                    if c >= 2:
                        sp.wait_ge(w_lo, c)
                    sp.dma_start(w_raw[:, c % 2, :], wo_t[c * P:(c + 1) * P, :]).then_inc(w_in[c % 2], 16)

                def load(b):
                    for k in range(ST):
                        after(sp, ot_lo, b * ST + (k - 1))
                        after(sp, xb_ready, b * ST + (k - 1))
                        carry(sp, ticks)
                        sp.dma_start(o_in[:, k % 2, :, :], ov[b, k]).then_inc(o_loaded[k % 2], 16)
                        sp.dma_start(x_in[:, k % 2, :], xv[b * ST + k]).then_inc(x_loaded[k % 2], 16)

                load(0)
                with sp.Fori(1, BATCH) as b:
                    load(b)

            @block.gpsimd
            def _(pool):
                make_identity(nc, pool, ident, s_id)
                pool.wait_ge(s_wide, 64)
                pool.wait_ge(s_gate, 5)
                nc.gpsimd.tensor_scalar(bo_wide[:, :], bo_wide[:, :], kept.gate[:, 0:1], None, ALU.mult)\
                    .then_inc(s_gbo, 1)
                pool.wait_ge(s_gbo, 1)

                def add_bias(i, half, slot):
                    pool.wait_ge(x_loaded[slot], half * 16 + 16)
                    after(pool, x1_ready, i)
                    nc.gpsimd.tensor_tensor(xb[:, :], x_in[:, slot, :], bo_wide[:, :], ALU.add).then_inc(xb_ready, 1)

                add_bias(0, 0, 0)

                def step(i, half, slot, last):
                    if not last:
                        add_bias(i + 1, half + slot, 1 - slot)
                    pool.wait_ge(gz_ready, i + 1)
                    after(pool, base_stored[slot], half * 16)
                    nc.gpsimd.tensor_tensor(base[:, slot, :], x1[:, :], gated_z[:, :], ALU.add)\
                        .then_inc(base_ready, 1)
                in_pairs(pool, TT, step)

            @block.scalar
            def _(act):
                act.wait_ge(s_wide, 64)
                nc.scalar.activation(kept.gate[:, :], kept.gate[:, :], ACT.Exp, scale=2.0).then_inc(s_gate, 1)
                act.wait_ge(r_in, 16)
                nc.scalar.copy(rt[0][:, :, :], rt_raw[:, :, :]).then_inc(w_hi, 1)
                for c in range(KC):
                    act.wait_ge(w_in[c % 2], 16 * (c // 2 + 1))
                    nc.scalar.copy(w[0][:, c, :], w_raw[:, c % 2, :]).then_inc(w_hi, 1)

                def high_of_values(i, half, slot):
                    act.wait_ge(o_loaded[slot], half * 16 + 16)
                    after(act, acc_ready, i - 1)
                    carry(act, ticks)
                    nc.scalar.copy(ot[0][:, slot, :, :], o_in[:, slot, :, :]).then_inc(ot_hi, 1)

                def high_of_h(i):
                    act.wait_ge(ht_ready, i + 1)
                    after(act, lg_ready, i)
                    carry(act, ticks)
                    nc.scalar.copy(ht[0][:, :, :], tp[:, :, :]).then_inc(ht_hi, 1)

                def exponentials(i):
                    act.wait_ge(lg_step, i * 4 + 4)
                    nc.scalar.activation(ex[:, :], top[:, 0:TOPK], ACT.Exp, bias=small[:, 4:5],
                                         accum_out=small[:, 5:6]).then_inc(s_ex, 1)

                def stores(i, slot):
                    act.wait_ge(base_ready, i + 1)
                    act.wait_ge(h_ready, i + 1)
                    carry(act, ticks)
                    act.dma_start(hv[i], h[:, slot, :]).then_inc(h_stored[slot], 16)
                    act.dma_start(bv[i], base[:, slot, :]).then_inc(base_stored[slot], 16)

                high_of_values(0, 0, 0)
                high_of_values(1, 0, 1)

                def step(i, half, slot, last):
                    if within(i + 2, TT):
                        high_of_values(i + 2, half + 1, slot)
                    if within(i - 1, TT):
                        high_of_h(i - 1)
                    act.wait_ge(s_var, i + 1)
                    nc.scalar.activation(small[:, 1:2], small[:, 0:1], ACT.Sqrt).then_inc(s_std, 1)
                    act.wait_ge(z_ready, i + 1)
                    nc.scalar.activation(zsq[:, :], z[:, :], ACT.Square, accum_out=small[:, 6:7]).then_inc(sq_ready, 1)
                    act.wait_ge(s_ms, i + 1)
                    nc.scalar.activation(small[:, 7:8], small[:, 2:3], ACT.Sqrt).then_inc(s_rms, 1)
                    stores(i, slot)
                    if within(i - 2, TT):
                        exponentials(i - 2)
                    if last:
                        exponentials(i - 1)
                        high_of_h(i)
                        exponentials(i)
                in_pairs(act, TT, step)
                for s in range(2):
                    act.wait_ge(h_stored[s], 16 * TT // 2)
                    act.wait_ge(base_stored[s], 16 * TT // 2)

            @block.vector
            def _(dve):
                dve.wait_ge(s_gate, 1)
                nc.vector.tensor_scalar(kept.gate[:, :], kept.gate[:, :], 1.0, None, ALU.add).then_inc(s_gate, 1)
                dve.wait_ge(s_gate, 2)
                nc.vector.reciprocal(kept.gate[:, :], kept.gate[:, :]).then_inc(s_gate, 1)
                dve.wait_ge(s_gate, 3)
                nc.vector.tensor_scalar(kept.gate[:, :], kept.gate[:, :], -2.0, 1.0, ALU.mult, ALU.add)\
                    .then_inc(s_gate, 2)
                dve.wait_ge(w_hi, 1)
                low_part(nc, rt[1][:, :, :], rt_raw[:, :, :], rt[0][:, :, :]).then_inc(w_lo, 1)
                for c in range(KC):
                    dve.wait_ge(w_hi, c + 2)
                    low_part(nc, w[1][:, c, :], w_raw[:, c % 2, :], w[0][:, c, :]).then_inc(w_lo, 1)
                dve.wait_ge(s_gbo, 1)

                def low_of_values(i, slot):
                    dve.wait_ge(ot_hi, i + 1)
                    low_part(nc, ot[1][:, slot, :, :], o_in[:, slot, :, :], ot[0][:, slot, :, :]).then_inc(ot_lo, 1)

                def add(i):
                    dve.wait_ge(acc_ready, i + 1)
                    dve.wait_ge(xb_ready, i + 1)
                    after(dve, base_ready, i)
                    nc.vector.scalar_tensor_tensor(x1[:, :], acc[:, :], kept.gate[:, 0:1], xb[:, :], ALU.mult,
                                                   ALU.add).then_inc(x1_ready, 1)

                def close(i, half, slot):
                    dve.wait_ge(x1_ready, i + 1)
                    nc.vector.bn_stats(stats[:, 0, :], x1[:, 0:DM // 2])
                    nc.vector.bn_stats(stats[:, 1, :], x1[:, DM // 2:DM]).then_inc(ln_step, 1)
                    dve.wait_ge(ln_step, i * 4 + 1)
                    carry(dve, ticks)
                    nc.vector.bn_aggr(mean_var[:, :], stats[:, :, :]).then_inc(ln_step, 1)
                    dve.wait_ge(ln_step, i * 4 + 2)
                    nc.vector.tensor_scalar(small[:, 0:1], mean_var[:, 1:2], LN_EPS, None, ALU.add).then_inc(s_var, 1)
                    dve.wait_ge(s_std, i + 1)
                    nc.vector.reciprocal(small[:, 1:2], small[:, 1:2]).then_inc(ln_step, 1)
                    dve.wait_ge(ln_step, i * 4 + 3)
                    nc.vector.tensor_scalar(z[:, :], x1[:, :], mean_var[:, 0:1], small[:, 1:2],
                                            ALU.subtract, ALU.mult).then_inc(z_ready, 1)
                    dve.wait_ge(z_ready, i + 1)
                    nc.vector.tensor_scalar(gated_z[:, :], z[:, :], kept.gate[:, 1:2], None, ALU.mult)\
                        .then_inc(gz_ready, 1)
                    dve.wait_ge(sq_ready, i + 1)
                    nc.vector.tensor_scalar(small[:, 2:3], small[:, 6:7], 1.0 / DM, RMS_EPS, ALU.mult, ALU.add)\
                        .then_inc(s_ms, 1)
                    dve.wait_ge(s_rms, i + 1)
                    nc.vector.reciprocal(small[:, 3:4], small[:, 7:8]).then_inc(ln_step, 1)
                    dve.wait_ge(ln_step, i * 4 + 4)
                    after(dve, h_stored[slot], half * 16)
                    nc.vector.scalar_tensor_tensor(h[:, slot, :], z[:, :], small[:, 3:4], nw_wide[:, :], ALU.mult,
                                                   ALU.mult).then_inc(h_ready, 1)

                def low_of_h(i):
                    dve.wait_ge(ht_hi, i + 1)
                    low_part(nc, ht[1][:, :, :], tp[:, :, :], ht[0][:, :, :]).then_inc(ht_lo, 1)

                def route(i):
                    dve.wait_ge(lg_ready, i + 1)
                    nc.vector.tensor_copy(logits[:, :], lg[:, :]).then_inc(lg_step, 1)
                    dve.wait_ge(lg_step, i * 4 + 1)
                    carry(dve, ticks)
                    nc.vector.max(top[:, :], logits[:, :]).then_inc(lg_step, 1)
                    dve.wait_ge(lg_step, i * 4 + 2)
                    carry(dve, ticks)
                    nc.vector.max_index(top_i[:, :], top[:, :], logits[:, :]).then_inc(lg_step, 1)
                    nc.vector.tensor_scalar(small[:, 4:5], top[:, 0:1], -1.0, None, ALU.mult).then_inc(lg_step, 1)
                    dve.wait_ge(lg_step, i * 4 + 3)
                    nc.vector.tensor_copy(kept.expert[:, i, :], top_i[:, 0:TOPK])
                    dve.wait_ge(s_ex, i + 1)
                    nc.vector.reciprocal(small[:, 5:6], small[:, 5:6]).then_inc(w_step, 1)
                    dve.wait_ge(w_step, i * 2 + 1)
                    nc.vector.tensor_scalar(kept.weights[:, i, :], ex[:, :], small[:, 5:6], kept.gate[:, 1:2],
                                            ALU.mult, ALU.mult).then_inc(w_step, 1)
                    dve.wait_ge(w_step, i * 2 + 2)

                low_of_values(0, 0)
                low_of_values(1, 1)

                def step(i, half, slot, last):
                    add(i)
                    if within(i + 2, TT):
                        low_of_values(i + 2, slot)
                    if within(i - 1, TT):
                        low_of_h(i - 1)
                    close(i, half, slot)
                    if within(i - 2, TT):
                        route(i - 2)
                    if last:
                        route(i - 1)
                        low_of_h(i)
                        route(i)
                in_pairs(dve, TT, step)

            @block.tensor
            def _(pe):
                pe.wait_ge(s_id, 2)

                def transpose_h(i, slot):
                    pe.wait_ge(h_ready, i + 1)
                    after(pe, ht_lo, i)
                    for c in range(KC):
                        done = nc.tensor.transpose(tp[:, c, :], h[:, slot, c * P:(c + 1) * P], ident[:, :])
                    done.then_inc(ht_ready, 1)

                def logits_of(i):
                    pe.wait_ge(ht_lo, i + 1)
                    after(pe, lg_step, i * 4)
                    for c in range(KC):
                        done = three_passes(nc, lg[:, :], [part[:, c, :] for part in ht],
                                            [part[:, c, :] for part in rt], c == 0, c == KC - 1)
                    done.then_inc(lg_ready, 1)

                pe.wait_ge(w_lo, KC + 1)

                def step(i, half, slot, last):
                    pe.wait_ge(ot_lo, i + 1)
                    after(pe, x1_ready, i)
                    for c in range(KC):
                        for n in range(2):
                            cols = slice(n * DM // 2, (n + 1) * DM // 2)
                            done = three_passes(nc, acc[:, cols], [part[:, slot, c, :] for part in ot],
                                                [part[:, c, cols] for part in w], c == 0, c == KC - 1)
                    done.then_inc(acc_ready, 1)
                    if within(i - 1, TT):
                        transpose_h(i - 1, 1 - slot)
                    if within(i - 2, TT):
                        logits_of(i - 2)
                    if last:
                        logits_of(i - 1)
                        transpose_h(i, slot)
                        logits_of(i)
                in_pairs(pe, TT, step)



def rank_tokens(nc, kept):
    with ExitStack() as ctx:
        t = Tools(nc, ctx, "r")
        ones = t.sb("ones", [P, P], BF16)
        before = t.sb("before", [P, P], BF16)
        iota_e = t.sb("iota_e", [P, NEXP], F32)
        hot = t.sb("hot", [P, TT, TOPK, NEXP], BF16)
        taken = t.sb("taken", [P, TT, NEXP], BF16)
        sums = t.sb("sums", [P, 2, TT + 1, NEXP], BF16)
        place = t.sb("place", [P, TT, NEXP], F32)
        pick = t.sb("pick", [P, TT, TOPK, NEXP], F32)
        slot_f = t.sb("slot_f", [P, TT, TOPK], F32)
        tile_f = t.sb("tile_f", [P, TT, TOPK], F32)
        tile_i = t.sb("tile_i", [P, TT, TOPK], I32)
        count = t.sb("count", [P, NEXP], F32)
        count_i = t.sb("count_i", [P, NEXP], I32)
        tiles = t.sb("tiles", [P, NEXP], F32)
        ends = t.sb("ends", [P, 2, NEXP], F32)
        first = t.sb("first", [P, NEXP], F32)
        bound_f = t.sb("bound_f", [1, NEXP + 1], F32)
        rank = t.ps("rank", [P, TT, NEXP])
        total = t.ps("total", [P, NEXP])
        s_c, s_v, s_p = t.sem("const"), t.sem("dve"), t.sem("pe")
        sums_at, sums_ready = [], []

        with nc.Block() as block:
            @block.gpsimd
            def _(pool):
                nc.gpsimd.memset(ones[:, :], 1.0).then_inc(s_c, 1)
                nc.gpsimd.iota(iota_e[:, :], pattern=[[1, NEXP]], base=0, channel_multiplier=0,
                               allow_small_or_imprecise_dtypes=True).then_inc(s_c, 1)
                pool.wait_ge(s_c, 2)
                nc.gpsimd.affine_select(out=before[:, :], in_=ones[:, :], compare_op=ALU.is_gt, fill=0.0, base=0,
                                        pattern=[[1, P]], channel_multiplier=-1).then_inc(s_c, 1)

            @block.vector
            def _(dve):
                n = [0]

                def link(ins):
                    n[0] += 1
                    ins.then_inc(s_v, 1)
                    dve.wait_ge(s_v, n[0])

                dve.wait_ge(s_c, 3)
                experts = kept.expert[:, :, :].rearrange("p n k -> p (n k)").unsqueeze(2)
                link(nc.vector.tensor_tensor(hot[:, :, :, :].rearrange("p n k e -> p (n k) e"),
                                             experts.to_broadcast([P, TT * TOPK, NEXP]),
                                             iota_e[:, :].unsqueeze(1).to_broadcast([P, TT * TOPK, NEXP]),
                                             ALU.is_equal))
                link(nc.vector.tensor_tensor(taken[:, :, :], hot[:, :, 0, :], hot[:, :, 1, :], ALU.add))
                for k in range(2, TOPK):
                    link(nc.vector.tensor_tensor(taken[:, :, :], taken[:, :, :], hot[:, :, k, :], ALU.add))
                link(nc.vector.memset(sums[:, 0, 0:1, :], 0.0))
                link(nc.vector.memset(sums[:, 1, 0:1, :], 0.0))
                link(nc.vector.tensor_copy(sums[:, 0, 1:TT + 1, :], taken[:, :, :]))
                at, step = 0, 1
                while step < TT + 1:
                    link(nc.vector.tensor_copy(sums[:, 1 - at, 0:step, :], sums[:, at, 0:step, :]))
                    link(nc.vector.tensor_tensor(sums[:, 1 - at, step:TT + 1, :], sums[:, at, step:TT + 1, :],
                                                 sums[:, at, 0:TT + 1 - step, :], ALU.add))
                    at, step = 1 - at, 2 * step
                sums_at.append(at)
                sums_ready.append(n[0])
                dve.wait_ge(s_p, 1)
                link(nc.vector.tensor_scalar(count[:, :], total[:, :], float(P - 1), None, ALU.add))
                link(nc.vector.tensor_copy(count_i[:, :], count[:, :]))
                link(nc.vector.tensor_scalar(count_i[:, :], count_i[:, :], 7, None, ALU.arith_shift_right))
                link(nc.vector.tensor_copy(tiles[:, :], count_i[:, :]))
                link(nc.vector.tensor_scalar(tiles[:, :], tiles[:, :], 2.0, None, ALU.max))
                link(nc.vector.tensor_copy(ends[:, 0, :], tiles[:, :]))
                at, step = 0, 1
                while step < NEXP:
                    link(nc.vector.tensor_copy(ends[:, 1 - at, 0:step], ends[:, at, 0:step]))
                    link(nc.vector.tensor_tensor(ends[:, 1 - at, step:NEXP], ends[:, at, step:NEXP],
                                                 ends[:, at, 0:NEXP - step], ALU.add))
                    at, step = 1 - at, 2 * step
                link(nc.vector.tensor_tensor(first[:, :], ends[:, at, :], tiles[:, :], ALU.subtract))
                link(nc.vector.memset(bound_f[0:1, 0:1], float(TT)))
                link(nc.vector.tensor_scalar(bound_f[0:1, 1:NEXP + 1], ends[0:1, at, :], float(TT), None,
                                             ALU.add))
                link(nc.vector.tensor_copy(kept.bounds[0:1, :], bound_f[0:1, :]))
                link(nc.vector.tensor_scalar(first[:, :], first[:, :], float(P), None, ALU.mult))
                link(nc.vector.tensor_tensor(place[:, :, :], rank[:, :, :],
                                             first[:, :].unsqueeze(1).to_broadcast([P, TT, NEXP]), ALU.add))
                for k in range(TOPK):
                    link(nc.vector.tensor_tensor(pick[:, :, k, :], hot[:, :, k, :], place[:, :, :], ALU.mult))
                link(nc.vector.tensor_reduce(slot_f[:, :, :].rearrange("p n k -> p (n k)"),
                                             pick[:, :, :, :].rearrange("p n k e -> p (n k) e"), AX.X, ALU.add))
                link(nc.vector.tensor_copy(kept.slots[:, :, :], slot_f[:, :, :]))
                link(nc.vector.tensor_scalar(tile_i[:, :, :], kept.slots[:, :, :], 7, None, ALU.arith_shift_right))
                link(nc.vector.tensor_scalar(kept.entries[:, :, :], kept.slots[:, :, :], P - 1, None,
                                             ALU.bitwise_and))
                link(nc.vector.tensor_copy(tile_f[:, :, :], tile_i[:, :, :]))
                link(nc.vector.tensor_copy(slot_f[:, :, :], kept.entries[:, :, :]))
                link(nc.vector.tensor_scalar(slot_f[:, :, :], slot_f[:, :, :], float(MAX_TILES), None, ALU.mult))
                link(nc.vector.tensor_tensor(slot_f[:, :, :], slot_f[:, :, :], tile_f[:, :, :], ALU.add))
                link(nc.vector.tensor_copy(kept.entries[:, :, :], slot_f[:, :, :]))

            @block.tensor
            def _(pe):
                pe.wait_ge(s_c, 3)
                pe.wait_ge(s_v, sums_ready[0])
                done_sums = sums[:, sums_at[0], :, :]
                half = TT // 2
                for u in range(2):
                    out = rank[:, u * half:(u + 1) * half, :]
                    nc.tensor.matmul(out, ones[:, :], done_sums[:, u * half:(u + 1) * half, :], start=True, stop=False)
                    nc.tensor.matmul(out, before[:, :], taken[:, u * half:(u + 1) * half, :], start=False, stop=True)
                nc.tensor.matmul(total[:, :], ones[:, :], done_sums[:, TT, :], start=True, stop=True).then_inc(s_p, 1)


def experts(nc, h_rows, base_rows, y_rows, w1_all, w2_all, table, kept, out):
    with ExitStack() as ctx:
        t_ = Tools(nc, ctx, "e")
        ticks = t_.sem("ticks")
        PARTS, RING = KC + FC, 4
        ROUTED_0, LAST = 1, SEGMENTS - 1
        ident = t_.sb("ident", [P, P], F32)
        w1 = [[t_.sb(f"w1_hi{s}", [P, KC, DM], F32R), t_.sb(f"w1_lo{s}", [P, KC, DM], F32R)] for s in range(2)]
        w2 = [t_.sb("w2_hi", [P, FC, DM], F32R), t_.sb("w2_lo", [P, FC, DM], F32R)]
        raw = t_.sb("raw", [P, RING, DM], F32)
        x = t_.sb("x", [P, DM], F32)
        xt = [t_.sb("xt_hi", [P, KC, P], F32R), t_.sb("xt_lo", [P, KC, P], F32R)]
        act_sb = t_.sb("act", [P, FF], F32)
        at = [t_.sb("at_hi", [P, FC, P], F32R), t_.sb("at_lo", [P, FC, P], F32R)]
        y_out = t_.sb("y_out", [P, DM], F32)
        base = t_.sb("base", [P, DM], F32)
        tokens = t_.sb("tokens", [P, MAX_TILES], I32)
        numbers = t_.sb("numbers", [P, TT], I32)
        entry = t_.sb("entry", [P, TOPK], I32)
        number = t_.sb("number", [P, 1], I32)
        index = t_.sb("index", [P, 1], I32)
        free = w1[1 - LAST % 2][0]
        rows = [free[:, k, :].bitcast(F32) for k in range(TOPK)]
        xt_ps = t_.ps("xt_ps", [P, KC, P])
        gu = t_.ps("gu", [P, 2, FF])
        at_ps = t_.ps("at_ps", [P, FC, P])
        y_ps = t_.ps("y_ps", [P, DM])
        hv = h_rows.rearrange("(n p) d -> n p d", p=P)
        bv = base_rows.rearrange("(n p) d -> n p d", p=P)
        yv = y_rows.rearrange("(n p) d -> n p d", p=P)
        outv = out.rearrange("(n p) d -> n p d", p=P)
        s_id = t_.sem("ident")
        w_in, w_hi, w_lo = t_.sems("w_in", RING), t_.sem("w_hi"), t_.sem("w_lo")
        x_in, xt_ready, x_hi, x_lo = t_.sem("x_in"), t_.sem("xt_ready"), t_.sem("x_hi"), t_.sem("x_lo")
        gu_ready, silu_ready, act_ready = t_.sem("gu_ready"), t_.sem("silu_ready"), t_.sem("act_ready")
        at_ready, a_hi, a_lo = t_.sem("at_ready"), t_.sem("a_hi"), t_.sem("a_lo")
        y_ready, y_left, y_right, y_stored = t_.sem("y_ready"), t_.sem("y_left"), t_.sem("y_right"), t_.sem("y_stored")
        base_in = t_.sem("base_in")
        s_table, s_numbers, s_entry, s_scattered = t_.sem("table"), t_.sem("numbers"), t_.sem("entry"), t_.sem("scattered")
        s_index, s_sum = t_.sem("index"), t_.sem("sum")
        s_fill, s_filled = t_.sem("fill"), t_.sem("filled")
        rows_in = t_.sems("rows_in", TOPK)
        HALF = DM // 2

        def segments(eng, step, close_segment):
            def shared(e, kind, kind_before, first):
                step(first, e, e % 2, True, kind, kind_before, 0)
                with eng.Fori(1, TT - 1) as n:
                    step(first + n, e, e % 2, False, kind, kind, n)
                step(first + (TT - 1), e, e % 2, False, kind, kind, TT - 1)
                close_segment(e, e % 2)

            def routed(e, slot, kind_before):
                begin = bound(eng, e - ROUTED_0)
                end = bound(eng, e - ROUTED_0 + 1)
                step(begin, e, slot, True, "routed", kind_before, None)
                with eng.Fori(begin + 1, end) as t:
                    step(t, e, slot, False, "routed", "routed", None)
                close_segment(e, slot)

            shared(0, "shared", None, 0)
            routed(1, 1, "shared")
            routed(2, 0, "routed")
            with eng.Fori(1, NEXP // 2) as j:
                routed(j * 2 + 1, 1, "routed")
                routed(j * 2 + 2, 0, "routed")
            first = bound(eng, NEXP)
            shared(LAST, "last", "routed", first)
            return first

        def bound(eng, j):
            least = TT + 2 * (j if isinstance(j, int) else 2)
            return eng.value_load(kept.bounds[0:1, bass.ds(j, 1)], min_val=least, max_val=TT + MAX_TILES)

        with nc.Block() as block:
            @block.sync
            def _(sp):
                def load(e, chunks):
                    for c in chunks:
                        after(sp, w_lo, e * PARTS + (c - (RING - 1)))
                        carry(sp, ticks)
                        src = w1_all[e, c * P:(c + 1) * P, :] if c < KC else w2_all[e, (c - KC) * P:(c - KC + 1) * P, :]
                        sp.dma_start(raw[:, c % RING, :], src).then_inc(w_in[c % RING], 16)

                load(0, range(PARTS))
                load(1, range(KC))
                first_free = bound(sp, NEXP)
                with sp.Fori(0, first_free):
                    sp.sem_inc(s_fill, 16)
                with sp.Fori(first_free, TT + MAX_TILES + 1) as t:
                    sp.wait_ge(s_fill, t * 16)
                    carry(sp, ticks)
                    sp.dma_start(yv[t - TT], hv[0]).then_inc(s_fill, 16)
                sp.wait_ge(s_fill, (TT + MAX_TILES + 1) * 16)
                sp.sem_inc(s_filled, 1)
                load(1, range(KC, PARTS))
                with sp.Fori(2, SEGMENTS) as e:
                    load(e, range(PARTS))

            @block.gpsimd
            def _(pool):
                make_identity(nc, pool, ident, s_id)
                nc.gpsimd.memset(tokens[:, :], 0).then_inc(s_numbers, 1)
                nc.gpsimd.iota(numbers[:, :], pattern=[[P, TT]], base=0, channel_multiplier=1).then_inc(s_numbers, 1)
                pool.wait_ge(s_numbers, 2)
                pool.dma_start(table.rearrange("(p n) o -> p (n o)", p=P), tokens[:, :]).then_inc(s_table, 16)
                pool.wait_ge(s_table, 16)

                def load_x(t, n):
                    after(pool, xt_ready, t * 2)
                    carry(pool, ticks)
                    pool.dma_start(x[:, :], hv[n]).then_inc(x_in, 16)

                def scatter(n):
                    after(pool, s_scattered, n * (16 * TOPK))
                    carry(pool, ticks)
                    nc.gpsimd.tensor_copy(entry[:, :], kept.entries[:, n, :])
                    nc.gpsimd.tensor_copy(number[:, :], numbers[:, bass.ds(n, 1)]).then_inc(s_entry, 1)
                    pool.wait_ge(s_entry, n + 1)
                    carry(pool, ticks)
                    for k in range(TOPK):
                        pool.indirect_dma_start(out=table, out_offset=bass.IndirectOffsetOnAxis(
                            ap=entry[:, k:k + 1], axis=0), in_=number[:, :], in_offset=None)\
                            .then_inc(s_scattered, 16)

                load_x(0, 0)
                scatter(0)
                with pool.Fori(1, TT) as n:
                    load_x(n, n)
                    scatter(n)
                pool.wait_ge(s_scattered, TT * 16 * TOPK)
                pool.dma_start(tokens[:, :], table.rearrange("(p n) o -> p (n o)", p=P)).then_inc(s_table, 16)
                pool.wait_ge(s_table, 32)

                first = bound(pool, NEXP)
                with pool.Fori(TT, first) as t:
                    pool.wait_ge(xt_ready, t * 2)
                    carry(pool, ticks)
                    nc.gpsimd.tensor_copy(index[:, :], tokens[:, bass.ds(t - TT, 1)]).then_inc(s_index, 1)
                    pool.wait_ge(s_index, t - (TT - 1))
                    carry(pool, ticks)
                    pool.indirect_dma_start(out=x[:, :], out_offset=None, in_=h_rows,
                                            in_offset=bass.IndirectOffsetOnAxis(ap=index[:, :], axis=0))\
                        .then_inc(x_in, 16)

                def gather(n):
                    after(pool, rows_in[TOPK - 1], n * 16)
                    carry(pool, ticks)
                    nc.gpsimd.tensor_copy(entry[:, :], kept.slots[:, n, :]).then_inc(s_entry, 1)
                    pool.wait_ge(s_entry, n + (TT + 1))
                    carry(pool, ticks)
                    for k in range(TOPK):
                        if within(n - 1, TT):
                            pool.wait_ge(s_sum, n * (TOPK + 1) + (k + 2 - (TOPK + 1)))
                            carry(pool, ticks)
                        pool.indirect_dma_start(out=rows[k], out_offset=None, in_=y_rows,
                                                in_offset=bass.IndirectOffsetOnAxis(ap=entry[:, k:k + 1], axis=0))\
                            .then_inc(rows_in[k], 16)

                for n in range(3):
                    load_x(first + n, n)
                pool.wait_ge(y_stored, first * 16 + 16)
                pool.wait_ge(s_filled, 1)
                carry(pool, ticks)
                gather(0)
                with pool.Fori(1, TT - 2) as n:
                    load_x(first + n + 2, n + 2)
                    gather(n)
                gather(TT - 2)
                gather(TT - 1)

            @block.scalar
            def _(act):
                def split(e, slot, c):
                    act.wait_ge(w_in[c % RING], e * (16 * PARTS // RING) + (16 * (c // RING) + 16))
                    dst = w1[slot][0][:, c, :] if c < KC else w2[0][:, c - KC, :]
                    nc.scalar.copy(dst, raw[:, c % RING, :]).then_inc(w_hi, 1)

                def high_of_x(t):
                    for u in range(2):
                        act.wait_ge(xt_ready, t * 2 + (u + 1))
                        cs = slice(u * KC // 2, (u + 1) * KC // 2)
                        nc.scalar.copy(xt[0][:, cs, :], xt_ps[:, cs, :]).then_inc(x_hi, 1)

                act.sem_inc(y_left, 1)
                act.sem_inc(y_stored, 16)

                def left_half(t, kind):
                    act.wait_ge(y_ready, t + 1)
                    act.wait_ge(y_stored, t * 16 + 16)
                    carry(act, ticks)
                    if kind == "routed":
                        nc.scalar.copy(y_out[:, 0:HALF], y_ps[:, 0:HALF]).then_inc(y_left, 1)
                    else:
                        act.sem_inc(y_left, 1)

                def store(t, kind, n):
                    act.wait_ge(y_left, t + 2)
                    act.wait_ge(y_right, t + 2)
                    carry(act, ticks)
                    dst = {"shared": bv, "routed": yv, "last": outv}[kind][t - TT if kind == "routed" else n]
                    act.dma_start(dst, y_out[:, :]).then_inc(y_stored, 16)

                def load_base(n):
                    act.dma_start(base[:, :], bv[n]).then_inc(base_in, 16)

                load_base(0)
                for c in range(KC):
                    split(0, 0, c)
                high_of_x(0)

                def step(t, e, slot, fresh, kind, before, n):
                    act.wait_ge(gu_ready, t + 1)
                    nc.scalar.activation(act_sb[:, :], gu[:, 0, :], ACT.Silu).then_inc(silu_ready, 1)
                    if not (kind == "last" and isinstance(n, int) and n == TT - 1):
                        high_of_x(t + 1)
                    if before:
                        left_half(t - 1, before)
                    act.wait_ge(at_ready, t + 1)
                    nc.scalar.copy(at[0][:, :, :], at_ps[:, :, :]).then_inc(a_hi, 1)
                    if before:
                        store(t - 1, before, None if before == "routed" else (TT - 1 if n is None else n - 1))
                        if kind != "routed":
                            load_base(n)
                    if fresh:
                        for c in range(KC, PARTS):
                            split(e, slot, c)
                        if not (isinstance(e, int) and e == LAST):
                            for c in range(KC // 2):
                                split(e + 1, 1 - slot, c)

                def close_segment(e, slot):
                    if not (isinstance(e, int) and e == LAST):
                        for c in range(KC // 2, KC):
                            split(e + 1, 1 - slot, c)

                first = segments(act, step, close_segment)
                left_half(first + (TT - 1), "last")
                store(first + (TT - 1), "last", TT - 1)
                act.wait_ge(y_stored, (first + TT) * 16 + 16)
                carry(act, ticks)

            @block.vector
            def _(dve):
                def split(e, slot, c):
                    dve.wait_ge(w_hi, e * PARTS + (c + 1))
                    w, k = (w1[slot], c) if c < KC else (w2, c - KC)
                    low_part(nc, w[1][:, k, :], raw[:, c % RING, :], w[0][:, k, :]).then_inc(w_lo, 1)

                def low_of_x(t):
                    for u in range(2):
                        dve.wait_ge(x_hi, t * 2 + (u + 1))
                        cs = slice(u * KC // 2, (u + 1) * KC // 2)
                        low_part(nc, xt[1][:, cs, :], xt_ps[:, cs, :], xt[0][:, cs, :]).then_inc(x_lo, 1)

                def finish(t, kind, n):
                    dve.wait_ge(y_ready, t + 1)
                    dve.wait_ge(y_stored, t * 16 + 16)
                    carry(dve, ticks)
                    if kind == "routed":
                        nc.vector.tensor_copy(y_out[:, HALF:DM], y_ps[:, HALF:DM]).then_inc(y_right, 1)
                        return
                    dve.wait_ge(base_in, (n + 1 + (TT if kind == "last" else 0)) * 16)
                    done = nc.vector.scalar_tensor_tensor(y_out[:, :], y_ps[:, :], kept.gate[:, 1:2], base[:, :],
                                                          ALU.mult, ALU.add)
                    if kind == "shared":
                        done.then_inc(y_right, 1)
                        return
                    done.then_inc(s_sum, 1)
                    for k in range(TOPK):
                        dve.wait_ge(s_sum, n * (TOPK + 1) + (k + 1))
                        dve.wait_ge(rows_in[k], (n + 1) * 16)
                        done = nc.vector.scalar_tensor_tensor(y_out[:, :], rows[k], kept.weights[:, n, k:k + 1],
                                                              y_out[:, :], ALU.mult, ALU.add).then_inc(s_sum, 1)
                    dve.wait_ge(s_sum, (n + 1) * (TOPK + 1))
                    dve.sem_inc(y_right, 1)

                dve.sem_inc(y_right, 1)
                for c in range(KC):
                    split(0, 0, c)
                low_of_x(0)

                def step(t, e, slot, fresh, kind, before, n):
                    dve.wait_ge(silu_ready, t + 1)
                    nc.vector.tensor_tensor(act_sb[:, :], act_sb[:, :], gu[:, 1, :], ALU.mult).then_inc(act_ready, 1)
                    if not (kind == "last" and isinstance(n, int) and n == TT - 1):
                        low_of_x(t + 1)
                    if before:
                        finish(t - 1, before, None if before == "routed" else (TT - 1 if n is None else n - 1))
                    dve.wait_ge(a_hi, t + 1)
                    low_part(nc, at[1][:, :, :], at_ps[:, :, :], at[0][:, :, :]).then_inc(a_lo, 1)
                    if fresh:
                        for c in range(KC, PARTS):
                            split(e, slot, c)
                        if not (isinstance(e, int) and e == LAST):
                            for c in range(KC // 2):
                                split(e + 1, 1 - slot, c)

                def close_segment(e, slot):
                    if not (isinstance(e, int) and e == LAST):
                        for c in range(KC // 2, KC):
                            split(e + 1, 1 - slot, c)

                first = segments(dve, step, close_segment)
                finish(first + (TT - 1), "last", TT - 1)

            @block.tensor
            def _(pe):
                def transpose_x(t):
                    pe.wait_ge(x_in, t * 16 + 16)
                    after(pe, x_lo, t * 2)
                    for c in range(KC):
                        done = nc.tensor.transpose(xt_ps[:, c, :], x[:, c * P:(c + 1) * P], ident[:, :])
                        if c % (KC // 2) == KC // 2 - 1:
                            done.then_inc(xt_ready, 1)

                def second_product(t):
                    pe.wait_ge(a_lo, t + 1)
                    pe.wait_ge(y_left, t + 1)
                    pe.wait_ge(y_right, t + 1)
                    for c in range(FC):
                        for n in range(2):
                            cols = slice(n * HALF, (n + 1) * HALF)
                            done = three_passes(nc, y_ps[:, cols], [part[:, c, :] for part in at],
                                                [part[:, c, cols] for part in w2], c == 0, c == FC - 1)
                    done.then_inc(y_ready, 1)

                pe.wait_ge(s_id, 2)
                transpose_x(0)

                def step(t, e, slot, fresh, kind, before, n):
                    pe.wait_ge(x_lo, t * 2 + 2)
                    after(pe, act_ready, t)
                    for c in range(KC):
                        if fresh:
                            pe.wait_ge(w_lo, e * PARTS + (c + 1))
                        for u in range(2):
                            done = three_passes(nc, gu[:, u, :], [part[:, c, :] for part in xt],
                                                [part[:, c, u * FF:(u + 1) * FF] for part in w1[slot]],
                                                c == 0, c == KC - 1)
                    done.then_inc(gu_ready, 1)
                    if not (kind == "last" and isinstance(n, int) and n == TT - 1):
                        transpose_x(t + 1)
                    if before:
                        if not fresh:
                            pe.wait_ge(w_lo, e * PARTS + PARTS)
                        second_product(t - 1)
                    pe.wait_ge(act_ready, t + 1)
                    after(pe, a_lo, t)
                    for c in range(FC):
                        done = nc.tensor.transpose(at_ps[:, c, :], act_sb[:, c * P:(c + 1) * P], ident[:, :])
                    done.then_inc(at_ready, 1)

                first = segments(pe, step, lambda e, slot: None)
                second_product(first + (TT - 1))


def program(nc, a, out):
    def scratch(name, shape, dt):
        return nc.dram_tensor(name, shape, dt, kind="Internal").ap()

    q_parts = scratch("q_parts", [BATCH * DM, 2, SEQ], F32)
    k_parts = scratch("k_parts", [BATCH * KV, 2, SEQ], F32)
    v_rows = scratch("v_rows", [BATCH, GROUPS, SEQ, HD], F32)
    o_cols = scratch("o_cols", [BATCH * DM, SEQ], F32)
    project_queries(nc, a["x"], a["wq_t"], a["bq_col"], q_parts)
    project_keys(nc, a["ctx_t"], a["wk_t"], a["wv_t"], a["bk_col"], a["bv"], k_parts, v_rows)
    h_rows = scratch("h_rows", [TOKENS, DM], F32)
    base_rows = scratch("base_rows", [TOKENS, DM], F32)
    attention(nc, q_parts, k_parts, v_rows, a["mask_s"], a["mask_st"], a["mask_b"], a["mask_b_col"], o_cols)
    with ExitStack() as ctx:
        kept = Kept(nc, ctx)
        close_attention(nc, a["x"], o_cols, a["wo_t"], a["bo"], a["norm_w"], a["router_t"],
                        (a["g_xattn"], a["g_ffn"]), h_rows, base_rows, kept)
        rank_tokens(nc, kept)
        experts(nc, h_rows, base_rows, scratch("y_rows", [(MAX_TILES + 1) * P, DM], F32), a["w1"], a["w2"],
                scratch("token_table", [P * MAX_TILES, 1], I32), kept, out)


def kernel(x, ctx_2048, mask_SxS2_bc0, mask_BxS2_bk0, g_xattn, g_ffn, L0_xattn_Wq, L0_xattn_bq, L0_xattn_Wk,
           L0_xattn_bk, L0_xattn_Wv, L0_xattn_bv, L0_xattn_Wo, L0_xattn_bo, L0_ffn_norm_w, L0_ffn_router_w,
           L0_ffn_w1, L0_ffn_w2, L0_ffn_sg, L0_ffn_su, L0_ffn_sd):
    import numpy as np
    import concourse.bacc as bacc
    from concourse.bass_utils import run_bass_kernel_spmd

    def c(v):
        return np.ascontiguousarray(v)

    sg, su, sd = (np.asarray(v) for v in (L0_ffn_sg, L0_ffn_su, L0_ffn_sd))

    def segments(shared, routed):
        return np.concatenate([shared(slice(0, FF))[None], routed, shared(slice(FF, 2 * FF))[None]], axis=0)

    mask_s = c(mask_SxS2_bc0)
    mask_b = c(mask_BxS2_bk0)
    arrays = {
        "x": c(x).reshape(TOKENS, DM), "ctx_t": c(np.transpose(np.asarray(ctx_2048), (0, 2, 1))),
        "mask_s": mask_s, "mask_st": c(mask_s.T), "mask_b": c(np.repeat(mask_b, GROUPS, axis=0)),
        "mask_b_col": c(np.repeat(mask_b.reshape(BATCH, ST, P).transpose(0, 2, 1), GROUPS, axis=0)),
        "g_xattn": c(g_xattn), "g_ffn": c(g_ffn),
        "wq_t": c(np.asarray(L0_xattn_Wq).T), "bq_col": c(np.asarray(L0_xattn_bq).reshape(KC, P).T),
        "wk_t": c(np.asarray(L0_xattn_Wk).T), "bk_col": c(np.asarray(L0_xattn_bk).reshape(KV // P, P).T),
        "wv_t": c(np.asarray(L0_xattn_Wv).T), "bv": c(L0_xattn_bv),
        "wo_t": c(np.asarray(L0_xattn_Wo).T), "bo": c(L0_xattn_bo),
        "norm_w": c(L0_ffn_norm_w), "router_t": c(np.asarray(L0_ffn_router_w).T),
        "w1": segments(lambda s: np.concatenate([sg[:, s], su[:, s]], axis=1), np.asarray(L0_ffn_w1)),
        "w2": segments(lambda s: sd[s], np.asarray(L0_ffn_w2)),
    }
    nc = bacc.Bacc("TRN2", target_bir_lowering=False, num_devices=1)
    aps = {n: nc.dram_tensor(f"in_{n}", v.shape, U8 if v.dtype == bool else mybir.dt.from_np(v.dtype),
                             kind="ExternalInput").ap()
           for n, v in arrays.items()}
    out = nc.dram_tensor("out", (TOKENS, DM), F32, kind="ExternalOutput").ap()
    program(nc, aps, out)
    r = run_bass_kernel_spmd(nc, [{f"in_{n}": v for n, v in arrays.items()}], core_ids=[0])
    return np.asarray(r.results[0]["out"]).reshape(BATCH, SEQ, DM)
```

```python
from contextlib import ExitStack

import concourse.bass as bass
from concourse import mybir

F32 = mybir.dt.float32
F32R = mybir.dt.float32r
BF16 = mybir.dt.bfloat16
I32 = mybir.dt.int32
U32 = mybir.dt.uint32
U8 = mybir.dt.uint8
ACT = mybir.ActivationFunctionType
ALU = mybir.AluOpType
AX = mybir.AxisListType

P = 128
BATCH, SEQ, DM = 8, 512, 1024
TOKENS = BATCH * SEQ
HEADS, GROUPS = 32, 8
HPG = HEADS // GROUPS
HD = DM // HEADS
KV = GROUPS * HD
NEXP, TOPK, FF = 32, 4, 512
KC = DM // P
FC = FF // P
ST = SEQ // P
TT = TOKENS // P
SEGMENTS = NEXP + 2
MAX_TILES = TOKENS * TOPK // P + 2 * NEXP
MASKED = -1.0e30
LN_EPS, RMS_EPS = 1e-5, 1e-6
SCALE = HD ** -0.5


class Tools:

    def __init__(self, nc, ctx, stage):
        self.nc, self.ctx, self.stage = nc, ctx, stage

    def sb(self, name, shape, dt):
        return self.ctx.enter_context(self.nc.sbuf_tensor(f"{self.stage}_{name}", shape, dt))

    def ps(self, name, shape, dt=F32):
        return self.ctx.enter_context(self.nc.psum_tensor(f"{self.stage}_{name}", shape, dt))

    def sem(self, name):
        return self.ctx.enter_context(self.nc.semaphore(f"{self.stage}_{name}"))

    def sems(self, name, n):
        return [self.sem(f"{name}{i}") for i in range(n)]


def carry(eng, ticks):
    eng.sem_inc(ticks, 1)


def after(eng, sem, count):
    if not (isinstance(count, int) and count <= 0):
        eng.wait_ge(sem, count)


def in_pairs(eng, n, body):
    body(0, 0, 0, False)
    body(1, 0, 1, False)
    with eng.Fori(1, n // 2 - 1) as j:
        body(j * 2, j, 0, False)
        body(j * 2 + 1, j, 1, False)
    body(n - 2, n // 2 - 1, 0, False)
    body(n - 1, n // 2 - 1, 1, True)


def in_fours(eng, n, body):
    for slot in range(4):
        body(slot, 0, slot)
    with eng.Fori(1, n // 4 - 1) as j:
        for slot in range(4):
            body(j * 4 + slot, j, slot)
    for slot in range(4):
        body(n - 4 + slot, n // 4 - 1, slot)


def within(i, n):
    return not isinstance(i, int) or 0 <= i < n


def three_passes(nc, out, a, b, first, last):
    nc.tensor.matmul(out, a[0], b[0], start=first, stop=False)
    nc.tensor.matmul(out, a[1], b[0], start=False, stop=False)
    return nc.tensor.matmul(out, a[0], b[1], start=False, stop=last)


def make_identity(nc, pool, ident, done):
    nc.gpsimd.memset(ident[:, :], 0.0).then_inc(done, 1)
    pool.wait_ge(done, 1)
    nc.gpsimd.affine_select(out=ident[:, :], in_=ident[:, :], compare_op=ALU.not_equal, fill=1.0,
                            base=0, pattern=[[-1, P]], channel_multiplier=1).then_inc(done, 1)


def low_part(nc, out, x, hi):
    return nc.vector.tensor_tensor(out, x, hi.bitcast(F32), ALU.subtract)


class ContextLoads:

    def __init__(self, nc, ctx):
        t = Tools(nc, ctx, "context")
        self.w_raw = t.sb("w_raw", [P, 2, KC, KV], F32)
        self.first = t.sb("first", [P, KC, SEQ], F32)
        self.w_in, self.loaded = t.sem("w_in"), t.sem("loaded")


def project_queries(nc, x, wq_t, bq_col, q_parts, context, ctx_t, wk_t, wv_t):
    with ExitStack() as ctx:
        t = Tools(nc, ctx, "q")
        ticks = t.sem("ticks")
        ident = t.sb("ident", [P, P], F32)
        w = [t.sb("w_hi", [P, KC, DM], F32R), t.sb("w_lo", [P, KC, DM], F32R)]
        w_raw = t.sb("w_raw", [P, 2, DM], F32)
        xt = [[t.sb(f"xt_hi{s}", [P, KC, SEQ], F32R), t.sb(f"xt_lo{s}", [P, KC, SEQ], F32R)] for s in range(2)]
        x_in = t.sb("x_in", [P, 2, DM], F32)
        xn = t.sb("xn", [P, 2, DM], F32)
        stats = t.sb("stats", [P, 2, 6], F32)
        mean_var = t.sb("mean_var", [P, 2], F32)
        var_eps = t.sb("var_eps", [P, 1], F32)
        std = t.sb("std", [P, 1], F32)
        rstd = t.sb("rstd", [P, 1], F32)
        bq = t.sb("bq", [P, KC], F32)
        q_out = t.sb("q_out", [P, 2, 2, SEQ], F32R)
        tp = [t.ps(f"tp{s}", [P, KC, P]) for s in range(2)]
        acc = [t.ps(f"acc{s}", [P, SEQ]) for s in range(2)]

        s_id, s_bq = t.sem("ident"), t.sem("bq")
        w_in, w_hi, w_lo = t.sems("w_in", 2), t.sem("w_hi"), t.sem("w_lo")
        x_loaded, xn_ready = t.sems("x_loaded", 2), t.sem("xn_ready")
        ln_step, s_var, s_std = t.sem("ln_step"), t.sem("var"), t.sem("std")
        tp_ready, tp_hi, tp_lo = t.sem("tp_ready"), t.sem("tp_hi"), t.sem("tp_lo")
        q_ready, q_hi, q_lo = t.sem("q_ready"), t.sem("q_hi"), t.sem("q_lo")
        q_stored = t.sems("q_stored", 2)
        xv = x.rearrange("(n p) d -> n p d", p=P)
        wv = wq_t.rearrange("(c p) f -> c p f", p=P)
        qv = q_parts.rearrange("(n p) h t -> n p h t", p=P)

        with nc.Block() as block:
            @block.sync
            def _(sp):
                sp.dma_start(bq[:, :], bq_col).then_inc(s_bq, 16)
                for n in range(2):
                    sp.dma_start(x_in[:, n, :], xv[n]).then_inc(x_loaded[n], 16)
                for c in range(KC):
                    after(sp, w_lo, c - 1)
                    sp.dma_start(w_raw[:, c % 2, :], wv[c]).then_inc(w_in[c % 2], 16)
                with sp.Fori(1, TT // 2) as j:
                    for s in range(2):
                        sp.wait_ge(xn_ready, j * 2 + (s - 1))
                        carry(sp, ticks)
                        sp.dma_start(x_in[:, s, :], xv[j * 2 + s]).then_inc(x_loaded[s], 16)
                for n, w_t in enumerate((wk_t, wv_t)):
                    sp.dma_start(context.w_raw[:, n, :, :], w_t.rearrange("(c p) f -> p c f", p=P))\
                        .then_inc(context.w_in, 16)
                sp.dma_start(context.first[:, :, :], ctx_t[0].rearrange("(c p) t -> p c t", p=P))\
                    .then_inc(context.loaded, 16)

            @block.gpsimd
            def _(pool):
                make_identity(nc, pool, ident, s_id)
                with pool.Fori(0, BATCH) as b:
                    for m in range(KC):
                        pool.wait_ge(q_lo, b * KC + (m + 1))
                        pool.dma_start(qv[b * KC + m], q_out[:, m % 2, :, :].bitcast(F32)).then_inc(q_stored[m % 2], 16)
                for s in range(2):
                    pool.wait_ge(q_stored[s], 16 * BATCH * KC // 2)

            @block.scalar
            def _(act):
                def root(n):
                    act.wait_ge(s_var, n + 1)
                    nc.scalar.activation(std[:, :], var_eps[:, :], ACT.Sqrt).then_inc(s_std, 1)

                def high_of_transposed(n, tile, slot):
                    act.wait_ge(tp_ready, n + 1)
                    nc.scalar.copy(xt[slot][0][:, :, tile * P:(tile + 1) * P], tp[tile % 2][:, :, :])\
                        .then_inc(tp_hi, 1)

                root(0)
                for c in range(KC):
                    act.wait_ge(w_in[c % 2], 16 * (c // 2 + 1))
                    nc.scalar.copy(w[0][:, c, :], w_raw[:, c % 2, :]).then_inc(w_hi, 1)
                for n in range(1, ST + 1):
                    root(n)
                    high_of_transposed(n - 1, n - 1, 0)
                act.wait_ge(s_bq, 16)

                def step(i, half, slot, last):
                    for k in range(ST):
                        if not last:
                            high_of_transposed(i * ST + (ST + k), k, 1 - slot)
                            if not (isinstance(i, int) and i * ST + ST + k + 1 >= TT):
                                root(i * ST + (ST + k + 1))
                        for m in (2 * k, 2 * k + 1):
                            act.wait_ge(q_ready, i * KC + (m + 1))
                            after(act, q_stored[m % 2], (i * (KC // 2) + m // 2) * 16)
                            nc.scalar.activation(q_out[:, m % 2, 0, :], acc[m % 2][:, :], ACT.Identity,
                                                 bias=bq[:, m:m + 1]).then_inc(q_hi, 1)
                in_pairs(act, BATCH, step)

            @block.vector
            def _(dve):
                def norm(n, half, slot):
                    dve.wait_ge(x_loaded[slot], half * 16 + 16)
                    after(dve, xn_ready, n)
                    nc.vector.bn_stats(stats[:, 0, :], x_in[:, slot, 0:DM // 2])
                    nc.vector.bn_stats(stats[:, 1, :], x_in[:, slot, DM // 2:DM]).then_inc(ln_step, 1)
                    dve.wait_ge(ln_step, n * 3 + 1)
                    carry(dve, ticks)
                    nc.vector.bn_aggr(mean_var[:, :], stats[:, :, :]).then_inc(ln_step, 1)
                    dve.wait_ge(ln_step, n * 3 + 2)
                    nc.vector.tensor_scalar(var_eps[:, :], mean_var[:, 1:2], LN_EPS, None, ALU.add)\
                        .then_inc(s_var, 1)
                    dve.wait_ge(s_std, n + 1)
                    nc.vector.reciprocal(rstd[:, :], std[:, :]).then_inc(ln_step, 1)
                    dve.wait_ge(ln_step, n * 3 + 3)
                    after(dve, tp_ready, n - 1)
                    nc.vector.tensor_scalar(xn[:, slot, :], x_in[:, slot, :], mean_var[:, 0:1], rstd[:, :],
                                            ALU.subtract, ALU.mult).then_inc(xn_ready, 1)

                def low_of_transposed(n, tile, slot):
                    dve.wait_ge(tp_hi, n + 1)
                    cols = slice(tile * P, (tile + 1) * P)
                    low_part(nc, xt[slot][1][:, :, cols], tp[tile % 2][:, :, :], xt[slot][0][:, :, cols])\
                        .then_inc(tp_lo, 1)

                norm(0, 0, 0)
                for c in range(KC):
                    dve.wait_ge(w_hi, c + 1)
                    low_part(nc, w[1][:, c, :], w_raw[:, c % 2, :], w[0][:, c, :]).then_inc(w_lo, 1)
                for n in range(1, ST + 1):
                    norm(n, n // 2, n % 2)
                    low_of_transposed(n - 1, n - 1, 0)
                dve.wait_ge(s_bq, 16)

                def step(i, half, slot, last):
                    for k in range(ST):
                        if not last:
                            low_of_transposed(i * ST + (ST + k), k, 1 - slot)
                            if not (isinstance(i, int) and i * ST + ST + k + 1 >= TT):
                                norm(i * ST + (ST + k + 1), i * (ST // 2) + (ST + k + 1) // 2, (k + 1) % 2)
                        for m in (2 * k, 2 * k + 1):
                            dve.wait_ge(q_hi, i * KC + (m + 1))
                            nc.vector.scalar_tensor_tensor(q_out[:, m % 2, 1, :], acc[m % 2][:, :], bq[:, m:m + 1],
                                                           q_out[:, m % 2, 0, :].bitcast(F32), ALU.add,
                                                           ALU.subtract).then_inc(q_lo, 1)
                in_pairs(dve, BATCH, step)

            @block.tensor
            def _(pe):
                pe.wait_ge(s_id, 2)

                def transpose_tile(n, tile):
                    pe.wait_ge(xn_ready, n + 1)
                    after(pe, tp_lo, n - 1)
                    for c in range(KC):
                        done = nc.tensor.transpose(tp[tile % 2][:, c, :], xn[:, tile % 2, c * P:(c + 1) * P],
                                                   ident[:, :])
                    done.then_inc(tp_ready, 1)

                for n in range(ST):
                    transpose_tile(n, n)
                pe.wait_ge(w_lo, KC)

                def step(i, half, slot, last):
                    for k in range(ST):
                        if not last:
                            transpose_tile(i * ST + (ST + k), k)
                        if k == 0:
                            pe.wait_ge(tp_lo, i * ST + ST)
                        for m in (2 * k, 2 * k + 1):
                            after(pe, q_lo, i * KC + (m - 1))
                            for c in range(KC):
                                done = three_passes(nc, acc[m % 2][:, :],
                                                    [part[:, c, m * P:(m + 1) * P] for part in w],
                                                    [part[:, c, :] for part in xt[slot]], c == 0, c == KC - 1)
                            done.then_inc(q_ready, 1)
                in_pairs(pe, BATCH, step)


def project_keys(nc, ctx_t, context, bk_col, bv_row, k_parts, v_rows):
    with ExitStack() as ctx:
        t = Tools(nc, ctx, "k")
        ticks = t.sem("ticks")
        wk = [t.sb("wk_hi", [P, KC, KV], F32R), t.sb("wk_lo", [P, KC, KV], F32R)]
        wv = [t.sb("wv_hi", [P, KC, KV], F32R), t.sb("wv_lo", [P, KC, KV], F32R)]
        w_raw = context.w_raw
        c_in = [context.first, t.sb("c_in1", [P, KC, SEQ], F32)]
        ct = [[t.sb(f"ct_hi{s}", [P, KC, SEQ], F32R), t.sb(f"ct_lo{s}", [P, KC, SEQ], F32R)] for s in range(2)]
        bk = t.sb("bk", [P, KV // P], F32)
        bv = t.sb("bv", [P, KV], F32)
        k_out = t.sb("k_out", [P, 2, 2, SEQ], F32R)
        v_out = t.sb("v_out", [P, 2, KV], F32)
        k_acc = [t.ps(f"k_acc{s}", [P, SEQ]) for s in range(2)]
        v_acc = [t.ps(f"v_acc{s}", [P, KV]) for s in range(2)]
        s_bias, w_in, w_hi, w_lo = t.sem("bias"), context.w_in, t.sem("w_hi"), t.sem("w_lo")
        c_loaded, c_hi, c_lo = [context.loaded, t.sem("c_loaded1")], t.sem("c_hi"), t.sem("c_lo")
        k_ready, k_hi, k_lo = t.sem("k_ready"), t.sem("k_hi"), t.sem("k_lo")
        v_ready, v_copied = t.sem("v_ready"), t.sem("v_copied")
        k_stored, v_stored = t.sems("k_stored", 2), t.sems("v_stored", 2)
        kv = k_parts.rearrange("(n p) h t -> n p h t", p=P)
        MK = KV // P
        cv = ctx_t.rearrange("b (c p) t -> b p c t", p=P)
        vv = v_rows.rearrange("b g (k p) d -> b k p g d", p=P)

        with nc.Block() as block:
            @block.sync
            def _(sp):
                sp.dma_start(bk[:, :], bk_col).then_inc(s_bias, 16)
                sp.dma_start(bv[:, :], bv_row.partition_broadcast(P)).then_inc(s_bias, 16)
                sp.dma_start(c_in[1][:, :, :], cv[1]).then_inc(c_loaded[1], 16)
                with sp.Fori(1, BATCH // 2) as j:
                    for s in range(2):
                        sp.wait_ge(c_lo, j * 2 + (s - 1))
                        carry(sp, ticks)
                        sp.dma_start(c_in[s][:, :, :], cv[j * 2 + s]).then_inc(c_loaded[s], 16)

            @block.gpsimd
            def _(pool):
                with pool.Fori(0, BATCH) as b:
                    for m in range(MK):
                        pool.wait_ge(k_lo, b * MK + (m + 1))
                        pool.dma_start(kv[b * MK + m], k_out[:, m, :, :].bitcast(F32)).then_inc(k_stored[m], 16)
                    for k in range(ST):
                        pool.wait_ge(v_copied, b * ST + (k + 1))
                        pool.dma_start(vv[b, k], v_out[:, k % 2, :].rearrange("p (g d) -> p g d", g=GROUPS))\
                            .then_inc(v_stored[k % 2], 16)
                for m in range(MK):
                    pool.wait_ge(k_stored[m], 16 * BATCH)
                for s in range(2):
                    pool.wait_ge(v_stored[s], 16 * BATCH * ST // 2)

            @block.scalar
            def _(act):
                act.wait_ge(w_in, 32)
                nc.scalar.copy(wk[0][:, :, :], w_raw[:, 0, :, :]).then_inc(w_hi, 1)
                nc.scalar.copy(wv[0][:, :, :], w_raw[:, 1, :, :]).then_inc(w_hi, 1)

                def high_of_context(i, half, slot):
                    act.wait_ge(c_loaded[slot], half * 16 + 16)
                    after(act, v_ready, i * ST - ST)
                    nc.scalar.copy(ct[slot][0][:, :, :], c_in[slot][:, :, :]).then_inc(c_hi, 1)

                high_of_context(0, 0, 0)
                act.wait_ge(s_bias, 32)

                def step(i, half, slot, last):
                    if not last:
                        high_of_context(i + 1, half + slot, 1 - slot)
                    for m in range(MK):
                        act.wait_ge(k_ready, i * MK + (m + 1))
                        after(act, k_stored[m], i * 16)
                        nc.scalar.activation(k_out[:, m, 0, :], k_acc[m][:, :], ACT.Identity,
                                             bias=bk[:, m:m + 1]).then_inc(k_hi, 1)
                in_pairs(act, BATCH, step)

            @block.vector
            def _(dve):
                for n, w in enumerate((wk, wv)):
                    dve.wait_ge(w_hi, n + 1)
                    low_part(nc, w[1][:, :, :], w_raw[:, n, :, :], w[0][:, :, :]).then_inc(w_lo, 1)

                def low_of_context(i, half, slot):
                    dve.wait_ge(c_hi, i + 1)
                    low_part(nc, ct[slot][1][:, :, :], c_in[slot][:, :, :], ct[slot][0][:, :, :]).then_inc(c_lo, 1)

                low_of_context(0, 0, 0)
                dve.wait_ge(s_bias, 32)

                def step(i, half, slot, last):
                    if not last:
                        low_of_context(i + 1, half + slot, 1 - slot)
                    for m in range(MK):
                        dve.wait_ge(k_hi, i * MK + (m + 1))
                        nc.vector.scalar_tensor_tensor(k_out[:, m, 1, :], k_acc[m][:, :], bk[:, m:m + 1],
                                                       k_out[:, m, 0, :].bitcast(F32), ALU.add,
                                                       ALU.subtract).then_inc(k_lo, 1)
                    for k in range(ST):
                        dve.wait_ge(v_ready, i * ST + (k + 1))
                        after(dve, v_stored[k % 2], (i * (ST // 2) + k // 2) * 16)
                        nc.vector.tensor_tensor(v_out[:, k % 2, :], v_acc[k % 2][:, :], bv[:, :], ALU.add)\
                            .then_inc(v_copied, 1)
                in_pairs(dve, BATCH, step)

            @block.tensor
            def _(pe):
                pe.wait_ge(w_lo, 2)

                def step(i, half, slot, last):
                    pe.wait_ge(c_lo, i + 1)
                    for m in range(MK):
                        after(pe, k_lo, i * MK + (m + 1 - MK))
                        for c in range(KC):
                            done = three_passes(nc, k_acc[m][:, :], [part[:, c, m * P:(m + 1) * P] for part in wk],
                                                [part[:, c, :] for part in ct[slot]], c == 0, c == KC - 1)
                        done.then_inc(k_ready, 1)
                    for k in range(ST):
                        after(pe, v_copied, i * ST + (k - 1))
                        for c in range(KC):
                            done = three_passes(nc, v_acc[k % 2][:, :],
                                                [part[:, c, k * P:(k + 1) * P] for part in ct[slot]],
                                                [part[:, c, :] for part in wv], c == 0, c == KC - 1)
                        done.then_inc(v_ready, 1)
                in_pairs(pe, BATCH, step)


def attention(nc, q_parts, k_parts, v_rows, mask_s, mask_st, mask_b, mask_b_col, o_cols, wo_t, w):
    with ExitStack() as ctx:
        t = Tools(nc, ctx, "a")
        ticks = t.sem("ticks")
        STEPS = BATCH * GROUPS
        SLOTS4 = 4
        NQ = HPG * ST
        GR = 2 * ST
        D3, ROWS = 3 * HD, 3 * HD + 2
        ident = t.sb("ident", [P, P], F32)
        ident_bf = t.sb("ident_bf", [P, P], BF16)
        qs = [t.sb(f"qs{s}", [ROWS, HPG, SEQ], F32R) for s in range(SLOTS4)]
        ks = [t.sb(f"ks{s}", [ROWS, SEQ], F32R) for s in range(SLOTS4)]
        vs = [t.sb(f"vs{s}", [P, ST, HD], F32) for s in range(SLOTS4)]
        ones = t.sb("ones", [P, HD], F32)
        ms_raw = t.sb("ms_raw", [P, ST, SEQ], U8)
        mst_raw = t.sb("mst_raw", [P, ST, SEQ], U8)
        ms = t.sb("ms", [P, ST, SEQ], BF16)
        mst = t.sb("mst", [P, ST, SEQ], BF16)
        mb_raw = t.sb("mb_raw", [P, BATCH, SEQ], U8)
        mb = t.sb("mb", [P, BATCH, SEQ], BF16)
        bias = t.sb("bias", [P, ST, SEQ], BF16)
        mbc_raw = t.sb("mbc_raw", [P, BATCH, ST], U8)
        mbc = t.sb("mbc", [P, BATCH, ST], F32)
        junk = t.sb("junk", [P, 2, SEQ], BF16)
        mx = t.sb("mx", [P, 2, NQ], F32)
        mt = t.sb("mt", [NQ, 2, 2, P], F32R)
        pt = t.sb("pt", [P, ST, HPG, SEQ], F32)
        w_raw = t.sb("w_raw", [P, 2, DM], F32)
        pt_sum = t.sb("pt_sum", [P, HPG, SEQ], F32)
        pv_sb = t.sb("pv_sb", [P, 2, SEQ], F32)
        rsum = t.sb("rsum", [P, 2, SEQ], F32)
        o_out = t.sb("o_out", [P, 2, SEQ], F32)
        s1 = [t.ps(f"s1_{s}", [P, SEQ]) for s in range(2)]
        s2 = [t.ps(f"s2_{s}", [P, 2, SEQ]) for s in range(2)]
        pv = t.ps("pv", [P, SEQ])
        total = t.ps("total", [P, SEQ])
        mtp = total[0:NQ, 0:P]
        s_id, s_mask, s_addend = t.sem("ident"), t.sem("mask"), t.sem("addend")
        s_ones = t.sem("ones")
        qk_in, v_in = t.sems("qk_in", SLOTS4), t.sems("v_in", SLOTS4)
        mb_in, mb_wide, bias_ready = t.sem("mb_in"), t.sem("mb_wide"), t.sem("bias_ready")
        s1_ready, s1_max = t.sem("s1_ready"), t.sem("s1_max")
        mt_ready, mt_hi, mt_lo, m_in = t.sem("mt_ready"), t.sem("mt_hi"), t.sem("mt_lo"), t.sems("m_in", SLOTS4)
        s2_ready, s_exp = t.sem("s2_ready"), t.sem("exp")
        pv_ready, pv_copied, pv_out = t.sem("pv_ready"), t.sem("pv_copied"), t.sem("pv_out")
        sum_step, total_ready, total_copied, total_inv = (t.sem(n) for n in (
            "sum_step", "total_ready", "total_copied", "total_inv"))
        w_in, w_hi, w_lo = t.sems("w_in", 2), t.sem("w_hi"), t.sem("w_lo")
        o_stored = t.sems("o_stored", 2)
        qv = q_parts.rearrange("(n r d) h t -> n h d r t", r=HPG, d=HD)
        kv = k_parts.rearrange("(n d) h t -> n h d t", d=HD)
        vv = v_rows.rearrange("b g (k p) d -> (b g) p k d", p=P)
        ov = o_cols.rearrange("(n p) t -> n p t", p=P)

        def ahead(quarter, slot, steps):
            return quarter + (slot + steps) // SLOTS4, (slot + steps) % SLOTS4

        def chunks(i):
            per_step = KC // SLOTS4
            return range(i * per_step, (i + 1) * per_step) if isinstance(i, int) and i < SLOTS4 else ()

        with nc.Block() as block:
            @block.sync
            def _(sp):
                sp.dma_start(ms_raw[:, :, :], mask_s.rearrange("(k p) t -> p k t", p=P)).then_inc(s_mask, 16)
                sp.dma_start(mst_raw[:, :, :], mask_st.rearrange("(k p) t -> p k t", p=P)).then_inc(s_mask, 16)

                sp.dma_start(mb_raw[:, :, :].rearrange("p b t -> p (b t)"),
                             mask_b.rearrange("b t -> (b t)").partition_broadcast(P)).then_inc(mb_in, 16)
                sp.dma_start(mbc_raw[:, :, :], mask_b_col).then_inc(mb_in, 16)

                def load(i, slot):
                    after(sp, s2_ready, (i - (SLOTS4 - 1)) * GR)
                    carry(sp, ticks)
                    for c, part in enumerate((0, 0, 1)):
                        sp.dma_start(qs[slot][c * HD:(c + 1) * HD, :, :].bitcast(F32), qv[i, part]).then_inc(qk_in[slot], 16)
                    for c, part in enumerate((0, 1, 0)):
                        sp.dma_start(ks[slot][c * HD:(c + 1) * HD, :].bitcast(F32), kv[i, part]).then_inc(qk_in[slot], 16)

                def load_values(i, slot):
                    after(sp, pv_ready, (i - (SLOTS4 - 1)) * ST)
                    carry(sp, ticks)
                    sp.dma_start(vs[slot][:, :, :], vv[i]).then_inc(v_in[slot], 16)

                def rows_of_maxima(i, slot):
                    sp.wait_ge(mt_lo, i + 1)
                    for part in range(2):
                        sp.dma_start(qs[slot][D3 + part:D3 + part + 1, :, :].bitcast(F32)
                                     .rearrange("o r (k p) -> o (r k) p", p=P),
                                     mt[:, slot % 2, part, :].bitcast(F32)).then_inc(m_in[slot], 16)

                for i in range(SLOTS4 - 1):
                    load(i, i)
                    load_values(i, i)
                rows_of_maxima(0, 0)

                def step(i, quarter, slot):
                    if within(i + 3, STEPS):
                        load(i + 3, (slot + 3) % SLOTS4)
                    if within(i + 1, STEPS):
                        rows_of_maxima(i + 1, (slot + 1) % SLOTS4)
                    if within(i + 3, STEPS):
                        load_values(i + 3, (slot + 3) % SLOTS4)
                    for c in chunks(i):
                        after(sp, w_lo, c - 1)
                        sp.dma_start(w_raw[:, c % 2, :], wo_t[c * P:(c + 1) * P, :]).then_inc(w_in[c % 2], 16)
                in_fours(sp, STEPS, step)

            @block.gpsimd
            def _(pool):
                make_identity(nc, pool, ident, s_id)
                pool.wait_ge(s_id, 2)
                nc.gpsimd.tensor_copy(ident_bf[:, :], ident[:, :]).then_inc(s_id, 1)
                pool.wait_ge(mb_in, 32)
                nc.gpsimd.tensor_scalar(mbc[:, :, :], mbc_raw[:, :, :], MASKED, None, ALU.mult).then_inc(mb_wide, 1)

                def step(i, quarter, slot):
                    for kt in range(1, ST):
                        pool.wait_ge(s_exp, i * GR + (2 * kt + 2))
                        if kt == 1:
                            after(pool, total_ready, i)
                        else:
                            pool.wait_ge(sum_step, i * (ST - 1) + (kt - 1))
                        carry(pool, ticks)
                        first = pt[:, 0, :, :] if kt == 1 else pt_sum[:, :, :]
                        nc.gpsimd.tensor_tensor(pt_sum[:, :, :], first, pt[:, kt, :, :], ALU.add).then_inc(sum_step, 1)
                in_fours(pool, STEPS, step)

            @block.scalar
            def _(act):
                def store(i, parity):
                    act.wait_ge(pv_out, i + 1)
                    carry(act, ticks)
                    act.dma_start(ov[i], o_out[:, parity, :]).then_inc(o_stored[parity], 16)

                def high_of_maxima(i, parity):
                    act.wait_ge(mt_ready, i + 1)
                    nc.scalar.mul(mt[:, parity, 0, :], mtp, -1.0).then_inc(mt_hi, 1)

                def copy_values(i, parity):
                    act.wait_ge(pv_ready, i * ST + ST)
                    after(act, pv_out, i - 1)
                    carry(act, ticks)
                    nc.scalar.copy(pv_sb[:, parity, :], pv[:, :]).then_inc(pv_copied, 1)

                def copy_sums(i, parity):
                    act.wait_ge(total_ready, i + 1)
                    nc.scalar.copy(rsum[:, parity, :], total[:, :]).then_inc(total_copied, 1)

                high_of_maxima(0, 0)

                act.wait_ge(mb_wide, 1)

                def step(i, quarter, slot):
                    batch = quarter // 2
                    for g in range(GR):
                        kt = g // 2
                        if g % 2 == 0:
                            after(act, pv_ready, i * ST + (kt + 1 - ST))
                            after(act, sum_step, i * (ST - 1) + (max(kt, 1) - (ST - 1)))
                        act.wait_ge(s2_ready, i * GR + (g + 1))
                        carry(act, ticks)
                        for v in range(2):
                            done = nc.scalar.activation(pt[:, kt, 2 * (g % 2) + v, :], s2[g % 2][:, v, :], ACT.Exp,
                                                        bias=mbc[:, batch, kt:kt + 1], scale=SCALE)
                        done.then_inc(s_exp, 1)
                        if g == 0 and within(i + 1, STEPS):
                            high_of_maxima(i + 1, (slot + 1) % 2)
                        if g >= GR - len(chunks(i)):
                            c = chunks(i)[g - GR]
                            act.wait_ge(w_in[c % 2], 16 * (c // 2 + 1))
                            nc.scalar.copy(w[0][:, c, :], w_raw[:, c % 2, :]).then_inc(w_hi, 1)
                        if g == 1 and within(i - 1, STEPS):
                            copy_values(i - 1, (slot + 1) % 2)
                        if g == GR - 1 and within(i - 2, STEPS):
                            store(i - 2, slot % 2)
                        if g == 4 and within(i - 1, STEPS):
                            copy_sums(i - 1, (slot + 1) % 2)
                    if not within(i + 1, STEPS):
                        store(i - 1, (slot + 1) % 2)
                        copy_values(i, slot % 2)
                        copy_sums(i, slot % 2)
                        store(i, slot % 2)
                in_fours(act, STEPS, step)
                for s in range(2):
                    act.wait_ge(o_stored[s], 16 * STEPS // 2)

            @block.vector
            def _(dve):
                def maxima(i, slot, n):
                    dve.wait_ge(s1_ready, i * NQ + (n + 1))
                    carry(dve, ticks)
                    nc.vector.tensor_tensor_reduce(out=junk[:, n % 2, :], in0=s1[n % 2][:, :],
                                                   in1=bias[:, n % ST, :], scale=1.0, scalar=-3.0e38,
                                                   op0=ALU.add, op1=ALU.max,
                                                   accum_out=mx[:, slot % 2, n:n + 1]).then_inc(s1_max, 1)

                def low_of_maxima(i, parity):
                    dve.wait_ge(mt_hi, i + 1)
                    nc.vector.scalar_tensor_tensor(mt[:, parity, 1, :], mtp, -1.0,
                                                   mt[:, parity, 0, :].bitcast(F32), ALU.mult, ALU.subtract)\
                        .then_inc(mt_lo, 1)

                def invert(i, parity, part):
                    if part == 0:
                        dve.wait_ge(total_copied, i + 1)
                    cols = slice(part * P, (part + 1) * P)
                    nc.vector.reciprocal(rsum[:, parity, cols], rsum[:, parity, cols]).then_inc(total_inv, 1)

                def normalise(i, quarter, slot):
                    dve.wait_ge(total_inv, i * ST + ST)
                    dve.wait_ge(pv_copied, i + 1)
                    after(dve, o_stored[slot % 2], quarter * 32 + (slot // 2) * 16)
                    carry(dve, ticks)
                    nc.vector.tensor_tensor(o_out[:, slot % 2, :], pv_sb[:, slot % 2, :], rsum[:, slot % 2, :], ALU.mult).then_inc(pv_out, 1)

                for s in range(SLOTS4):
                    nc.vector.memset(ks[s][D3:ROWS, :].bitcast(F32), 1.0).then_inc(s_ones, 1)
                nc.vector.memset(ones[:, :], 1.0).then_inc(s_ones, 1)
                def addends(batch, count):
                    carry(dve, ticks)
                    nc.vector.tensor_tensor(bias[:, :, :], ms[:, :, :],
                                            mb[:, batch, :].unsqueeze(1).to_broadcast([P, ST, SEQ]), ALU.add)\
                        .then_inc(bias_ready, 1)
                    dve.wait_ge(bias_ready, count)

                dve.wait_ge(s_mask, 32)
                nc.vector.tensor_scalar(ms[:, :, :], ms_raw[:, :, :], MASKED, None, ALU.mult).then_inc(s_addend, 1)
                dve.wait_ge(mb_in, 32)
                nc.vector.tensor_scalar(mb[:, :, :], mb_raw[:, :, :], MASKED, None, ALU.mult).then_inc(s_addend, 1)
                nc.vector.tensor_scalar(mst[:, :, :], mst_raw[:, :, :], MASKED, None, ALU.mult).then_inc(s_addend, 1)
                dve.wait_ge(s_addend, 3)
                addends(0, 1)
                for i in range(2):
                    for n in range(NQ):
                        maxima(i, i, n)
                    if i == 0:
                        low_of_maxima(0, 0)

                def step(i, quarter, slot):
                    if slot == 2 and within(i + 2, STEPS):
                        dve.wait_ge(s1_max, (i + 2) * NQ)
                        addends((quarter + 1) // 2, quarter + 2)
                    if within(i + 1, STEPS):
                        low_of_maxima(i + 1, (slot + 1) % 2)
                    for n in range(NQ):
                        if n in (2, 6) and within(i - 2, STEPS):
                            invert(i - 2, slot % 2, 2 + n // 6)
                        if n == 8 and within(i - 2, STEPS):
                            normalise(i - 2, *ahead(quarter, slot, -2))
                        if n in (10, 14) and within(i - 1, STEPS):
                            invert(i - 1, (slot + 1) % 2, n // 14)
                        if within(i + 2, STEPS):
                            maxima(i + 2, (slot + 2) % SLOTS4, n)
                    for c in chunks(i):
                        dve.wait_ge(w_hi, c + 1)
                        low_part(nc, w[1][:, c, :], w_raw[:, c % 2, :], w[0][:, c, :]).then_inc(w_lo, 1)
                    if not within(i + 1, STEPS):
                        for part in range(2, ST):
                            invert(i - 1, (slot + 1) % 2, part)
                        normalise(i - 1, *ahead(quarter, slot, -1))
                        for part in range(ST):
                            invert(i, slot % 2, part)
                        normalise(i, quarter, slot)
                in_fours(dve, STEPS, step)

            @block.tensor
            def _(pe):
                def scores_of_queries(i, slot, n):
                    after(pe, s1_max, i * NQ + (n - 1))
                    qt = n % ST
                    nc.tensor.matmul(s1[n % 2][:, :], qs[slot][0:D3, n // ST, qt * P:(qt + 1) * P], ks[slot][0:D3, :],
                                     start=True, stop=True).then_inc(s1_ready, 1)

                def operands(quarter, slot):
                    pe.wait_ge(qk_in[slot], quarter * 96 + 96)

                def transpose_maxima(i, parity):
                    pe.wait_ge(s1_max, i * NQ + NQ)
                    after(pe, total_copied, i - 2)
                    nc.tensor.transpose(mtp, mx[:, parity, :], ident[:, :]).then_inc(mt_ready, 1)

                def scores_of_keys(i, slot, g):
                    after(pe, s_exp, i * GR + (g - 1))
                    kt = g // 2
                    for v in range(2):
                        nc.tensor.matmul(s2[g % 2][:, v, :], ks[slot][:, kt * P:(kt + 1) * P],
                                         qs[slot][:, 2 * (g % 2) + v, :], start=True, stop=False)
                        done = nc.tensor.matmul(s2[g % 2][:, v, :], ident_bf[:, :], mst[:, kt, :], start=False,
                                                stop=True)
                    done.then_inc(s2_ready, 1)

                def column_tiles(out, weights, p, start, stop):
                    for r in range(HPG):
                        done = nc.tensor.matmul(out[r * HD:(r + 1) * HD, :], weights, p[:, r, :],
                                                start=start, stop=stop, tile_position=(0, r * HD))
                    return done

                def values(i, quarter, slot, kt):
                    pe.wait_ge(s_exp, i * GR + (2 * kt + 2))
                    if kt == 0:
                        pe.wait_ge(v_in[slot], quarter * 16 + 16)
                        after(pe, pv_copied, i)
                    column_tiles(pv, vs[slot][:, kt, :], pt[:, kt, :, :], kt == 0, kt == ST - 1).then_inc(pv_ready, 1)

                def sums(i):
                    pe.wait_ge(sum_step, (i + 1) * (ST - 1))
                    after(pe, total_copied, i)
                    pe.wait_ge(mt_lo, min(i + 3, STEPS) if isinstance(i, int) else i + 3)
                    column_tiles(total, ones[:, :], pt_sum, True, True).then_inc(total_ready, 1)

                pe.wait_ge(s_id, 3)
                pe.wait_ge(s_ones, SLOTS4 + 1)
                pe.wait_ge(s_addend, 3)
                operands(0, 0)
                for n in range(NQ):
                    scores_of_queries(0, 0, n)
                transpose_maxima(0, 0)
                operands(0, 1)
                for n in range(NQ):
                    scores_of_queries(1, 1, n)

                def step(i, quarter, slot):
                    pe.wait_ge(m_in[slot], quarter * 32 + 32)
                    later = within(i + 2, STEPS)
                    if later:
                        operands(*ahead(quarter, slot, 2))
                    queries = iter(range(NQ if later else 0))

                    def some_queries(count):
                        for _ in range(count):
                            n = next(queries, None)
                            if n is not None:
                                scores_of_queries(i + 2, (slot + 2) % SLOTS4, n)

                    for kt in range(ST):
                        scores_of_keys(i, slot, 2 * kt)
                        some_queries(1)
                        scores_of_keys(i, slot, 2 * kt + 1)
                        if kt == 0 and within(i + 1, STEPS):
                            transpose_maxima(i + 1, (slot + 1) % 2)
                        some_queries(1)
                        before = (i, quarter, slot, kt - 1) if kt else (i - 1, *ahead(quarter, slot, -1), ST - 1)
                        if within(before[0], STEPS):
                            values(*before)
                        some_queries(1)
                        if kt == 1 and within(i - 1, STEPS):
                            sums(i - 1)
                        some_queries(1)
                    if not within(i + 1, STEPS):
                        values(i, quarter, slot, ST - 1)
                        sums(i)
                in_fours(pe, STEPS, step)


class Kept:

    def __init__(self, nc, ctx):
        t = Tools(nc, ctx, "kept")
        self.slots = t.sb("slots", [P, TT, TOPK], I32)
        self.entries = t.sb("entries", [P, TT, TOPK], I32)
        self.weights = t.sb("weights", [P, TT, TOPK], F32)
        self.expert = t.sb("expert", [P, TT, TOPK], F32)
        self.bounds = t.sb("bounds", [1, NEXP + 1], I32)
        self.gate = t.sb("gate", [P, 2], F32)


def close_attention(nc, x, o_cols, w, bo, norm_w, router_t, gates, h_rows, base_rows, kept):
    with ExitStack() as ctx:
        t = Tools(nc, ctx, "c")
        ticks = t.sem("ticks")
        ident = t.sb("ident", [P, P], F32)
        rt = [t.sb("rt_hi", [P, KC, NEXP], F32R), t.sb("rt_lo", [P, KC, NEXP], F32R)]
        rt_raw = t.sb("rt_raw", [P, KC, NEXP], F32)
        o_in = t.sb("o_in", [P, 2, KC, P], F32)
        x_in = t.sb("x_in", [P, 2, DM], F32)
        bo_wide = t.sb("bo_wide", [P, DM], F32)
        nw_wide = t.sb("nw_wide", [P, DM], F32)
        xb = t.sb("xb", [P, DM], F32)
        ot = [t.sb("ot_hi", [P, 2, KC, P], F32R), t.sb("ot_lo", [P, 2, KC, P], F32R)]
        ht = [t.sb("ht_hi", [P, KC, P], F32R), t.sb("ht_lo", [P, KC, P], F32R)]
        x1 = t.sb("x1", [P, DM], F32)
        z = t.sb("z", [P, DM], F32)
        zsq = t.sb("zsq", [P, DM], BF16)
        h = t.sb("h", [P, 2, DM], F32)
        base = t.sb("base", [P, 2, DM], F32)
        gated_z = t.sb("gated_z", [P, DM], F32)
        stats = t.sb("stats", [P, 2, 6], F32)
        mean_var = t.sb("mean_var", [P, 2], F32)
        small = t.sb("small", [P, 8], F32)
        logits = t.sb("logits", [P, NEXP], F32)
        top = t.sb("top", [P, 8], F32)
        top_i = t.sb("top_i", [P, 8], U32)
        ex = t.sb("ex", [P, TOPK], F32)
        tp = t.ps("tp", [P, KC, P])
        acc = t.ps("acc", [P, DM])
        lg = t.ps("lg", [P, NEXP])
        xv = x.rearrange("(n p) d -> n p d", p=P)
        ov = o_cols.rearrange("(b c p) (k t) -> b k p c t", c=KC, p=P, t=P)
        hv = h_rows.rearrange("(n p) d -> n p d", p=P)
        bv = base_rows.rearrange("(n p) d -> n p d", p=P)
        s_id, s_wide, s_gate, s_gbo = t.sem("ident"), t.sem("wide"), t.sem("gate"), t.sem("gbo")
        r_in, r_hi, r_lo = t.sem("r_in"), t.sem("r_hi"), t.sem("r_lo")
        o_loaded, x_loaded = t.sems("o_loaded", 2), t.sems("x_loaded", 2)
        xb_ready = t.sem("xb_ready")
        ot_hi, ot_lo = t.sem("ot_hi"), t.sem("ot_lo")
        acc_ready, x1_ready = t.sem("acc_ready"), t.sem("x1_ready")
        ln_step, s_var, s_std, z_ready = t.sem("ln_step"), t.sem("var"), t.sem("std"), t.sem("z_ready")
        sq_ready, s_ms, s_rms, h_ready = t.sem("sq_ready"), t.sem("ms"), t.sem("rms"), t.sem("h_ready")
        gz_ready, base_ready = t.sem("gz_ready"), t.sem("base_ready")
        ht_ready, ht_hi, ht_lo = t.sem("ht_ready"), t.sem("ht_hi"), t.sem("ht_lo")
        lg_ready, lg_step, s_ex, w_step = t.sem("lg_ready"), t.sem("lg_step"), t.sem("ex"), t.sem("w_step")
        h_stored, base_stored = t.sems("h_stored", 2), t.sems("base_stored", 2)

        with nc.Block() as block:
            @block.sync
            def _(sp):
                sp.dma_start(kept.gate[:, 0:1], gates[0].partition_broadcast(P)).then_inc(s_wide, 16)
                sp.dma_start(kept.gate[:, 1:2], gates[1].partition_broadcast(P)).then_inc(s_wide, 16)
                sp.dma_start(bo_wide[:, :], bo.partition_broadcast(P)).then_inc(s_wide, 16)
                sp.dma_start(nw_wide[:, :], norm_w.partition_broadcast(P)).then_inc(s_wide, 16)
                sp.dma_start(rt_raw[:, :, :], router_t.rearrange("(c p) e -> p c e", p=P)).then_inc(r_in, 16)

                def load(b):
                    for k in range(ST):
                        after(sp, ot_lo, b * ST + (k - 1))
                        after(sp, xb_ready, b * ST + (k - 1))
                        carry(sp, ticks)
                        sp.dma_start(o_in[:, k % 2, :, :], ov[b, k]).then_inc(o_loaded[k % 2], 16)
                        sp.dma_start(x_in[:, k % 2, :], xv[b * ST + k]).then_inc(x_loaded[k % 2], 16)

                load(0)
                with sp.Fori(1, BATCH) as b:
                    load(b)

            @block.gpsimd
            def _(pool):
                make_identity(nc, pool, ident, s_id)
                pool.wait_ge(s_wide, 64)
                pool.wait_ge(s_gate, 5)
                nc.gpsimd.tensor_scalar(bo_wide[:, :], bo_wide[:, :], kept.gate[:, 0:1], None, ALU.mult)\
                    .then_inc(s_gbo, 1)
                pool.wait_ge(s_gbo, 1)

                def add_bias(i, half, slot):
                    pool.wait_ge(x_loaded[slot], half * 16 + 16)
                    after(pool, x1_ready, i)
                    nc.gpsimd.tensor_tensor(xb[:, :], x_in[:, slot, :], bo_wide[:, :], ALU.add).then_inc(xb_ready, 1)

                add_bias(0, 0, 0)

                def step(i, half, slot, last):
                    if not last:
                        add_bias(i + 1, half + slot, 1 - slot)
                    pool.wait_ge(gz_ready, i + 1)
                    after(pool, base_stored[slot], half * 16)
                    nc.gpsimd.tensor_tensor(base[:, slot, :], x1[:, :], gated_z[:, :], ALU.add)\
                        .then_inc(base_ready, 1)
                in_pairs(pool, TT, step)

            @block.scalar
            def _(act):
                act.wait_ge(s_wide, 64)
                nc.scalar.activation(kept.gate[:, :], kept.gate[:, :], ACT.Exp, scale=2.0).then_inc(s_gate, 1)
                act.wait_ge(r_in, 16)
                nc.scalar.copy(rt[0][:, :, :], rt_raw[:, :, :]).then_inc(r_hi, 1)

                def high_of_values(i, half, slot):
                    act.wait_ge(o_loaded[slot], half * 16 + 16)
                    after(act, acc_ready, i - 1)
                    carry(act, ticks)
                    nc.scalar.copy(ot[0][:, slot, :, :], o_in[:, slot, :, :]).then_inc(ot_hi, 1)

                def high_of_h(i):
                    act.wait_ge(ht_ready, i + 1)
                    after(act, lg_ready, i)
                    carry(act, ticks)
                    nc.scalar.copy(ht[0][:, :, :], tp[:, :, :]).then_inc(ht_hi, 1)

                def exponentials(i):
                    act.wait_ge(lg_step, i * 4 + 4)
                    nc.scalar.activation(ex[:, :], top[:, 0:TOPK], ACT.Exp, bias=small[:, 4:5],
                                         accum_out=small[:, 5:6]).then_inc(s_ex, 1)

                def stores(i, slot):
                    act.wait_ge(base_ready, i + 1)
                    act.wait_ge(h_ready, i + 1)
                    carry(act, ticks)
                    act.dma_start(hv[i], h[:, slot, :]).then_inc(h_stored[slot], 16)
                    act.dma_start(bv[i], base[:, slot, :]).then_inc(base_stored[slot], 16)

                high_of_values(0, 0, 0)
                high_of_values(1, 0, 1)

                def step(i, half, slot, last):
                    if within(i + 2, TT):
                        high_of_values(i + 2, half + 1, slot)
                    if within(i - 1, TT):
                        high_of_h(i - 1)
                    act.wait_ge(s_var, i + 1)
                    nc.scalar.activation(small[:, 1:2], small[:, 0:1], ACT.Sqrt).then_inc(s_std, 1)
                    act.wait_ge(z_ready, i + 1)
                    nc.scalar.activation(zsq[:, :], z[:, :], ACT.Square, accum_out=small[:, 6:7]).then_inc(sq_ready, 1)
                    act.wait_ge(s_ms, i + 1)
                    nc.scalar.activation(small[:, 7:8], small[:, 2:3], ACT.Sqrt).then_inc(s_rms, 1)
                    stores(i, slot)
                    if within(i - 2, TT):
                        exponentials(i - 2)
                    if last:
                        exponentials(i - 1)
                        high_of_h(i)
                        exponentials(i)
                in_pairs(act, TT, step)
                for s in range(2):
                    act.wait_ge(h_stored[s], 16 * TT // 2)
                    act.wait_ge(base_stored[s], 16 * TT // 2)

            @block.vector
            def _(dve):
                dve.wait_ge(s_gate, 1)
                nc.vector.tensor_scalar(kept.gate[:, :], kept.gate[:, :], 1.0, None, ALU.add).then_inc(s_gate, 1)
                dve.wait_ge(s_gate, 2)
                nc.vector.reciprocal(kept.gate[:, :], kept.gate[:, :]).then_inc(s_gate, 1)
                dve.wait_ge(s_gate, 3)
                nc.vector.tensor_scalar(kept.gate[:, :], kept.gate[:, :], -2.0, 1.0, ALU.mult, ALU.add)\
                    .then_inc(s_gate, 2)
                dve.wait_ge(r_hi, 1)
                low_part(nc, rt[1][:, :, :], rt_raw[:, :, :], rt[0][:, :, :]).then_inc(r_lo, 1)
                dve.wait_ge(s_gbo, 1)

                def low_of_values(i, slot):
                    dve.wait_ge(ot_hi, i + 1)
                    low_part(nc, ot[1][:, slot, :, :], o_in[:, slot, :, :], ot[0][:, slot, :, :]).then_inc(ot_lo, 1)

                def add(i):
                    dve.wait_ge(acc_ready, i + 1)
                    dve.wait_ge(xb_ready, i + 1)
                    after(dve, base_ready, i)
                    nc.vector.scalar_tensor_tensor(x1[:, :], acc[:, :], kept.gate[:, 0:1], xb[:, :], ALU.mult,
                                                   ALU.add).then_inc(x1_ready, 1)

                def close(i, half, slot):
                    dve.wait_ge(x1_ready, i + 1)
                    nc.vector.bn_stats(stats[:, 0, :], x1[:, 0:DM // 2])
                    nc.vector.bn_stats(stats[:, 1, :], x1[:, DM // 2:DM]).then_inc(ln_step, 1)
                    dve.wait_ge(ln_step, i * 4 + 1)
                    carry(dve, ticks)
                    nc.vector.bn_aggr(mean_var[:, :], stats[:, :, :]).then_inc(ln_step, 1)
                    dve.wait_ge(ln_step, i * 4 + 2)
                    nc.vector.tensor_scalar(small[:, 0:1], mean_var[:, 1:2], LN_EPS, None, ALU.add).then_inc(s_var, 1)
                    dve.wait_ge(s_std, i + 1)
                    nc.vector.reciprocal(small[:, 1:2], small[:, 1:2]).then_inc(ln_step, 1)
                    dve.wait_ge(ln_step, i * 4 + 3)
                    nc.vector.tensor_scalar(z[:, :], x1[:, :], mean_var[:, 0:1], small[:, 1:2],
                                            ALU.subtract, ALU.mult).then_inc(z_ready, 1)
                    dve.wait_ge(z_ready, i + 1)
                    nc.vector.tensor_scalar(gated_z[:, :], z[:, :], kept.gate[:, 1:2], None, ALU.mult)\
                        .then_inc(gz_ready, 1)
                    dve.wait_ge(sq_ready, i + 1)
                    nc.vector.tensor_scalar(small[:, 2:3], small[:, 6:7], 1.0 / DM, RMS_EPS, ALU.mult, ALU.add)\
                        .then_inc(s_ms, 1)
                    dve.wait_ge(s_rms, i + 1)
                    nc.vector.reciprocal(small[:, 3:4], small[:, 7:8]).then_inc(ln_step, 1)
                    dve.wait_ge(ln_step, i * 4 + 4)
                    after(dve, h_stored[slot], half * 16)
                    nc.vector.scalar_tensor_tensor(h[:, slot, :], z[:, :], small[:, 3:4], nw_wide[:, :], ALU.mult,
                                                   ALU.mult).then_inc(h_ready, 1)

                def low_of_h(i):
                    dve.wait_ge(ht_hi, i + 1)
                    low_part(nc, ht[1][:, :, :], tp[:, :, :], ht[0][:, :, :]).then_inc(ht_lo, 1)

                def route(i):
                    dve.wait_ge(lg_ready, i + 1)
                    nc.vector.tensor_copy(logits[:, :], lg[:, :]).then_inc(lg_step, 1)
                    dve.wait_ge(lg_step, i * 4 + 1)
                    carry(dve, ticks)
                    nc.vector.max(top[:, :], logits[:, :]).then_inc(lg_step, 1)
                    dve.wait_ge(lg_step, i * 4 + 2)
                    carry(dve, ticks)
                    nc.vector.max_index(top_i[:, :], top[:, :], logits[:, :]).then_inc(lg_step, 1)
                    nc.vector.tensor_scalar(small[:, 4:5], top[:, 0:1], -1.0, None, ALU.mult).then_inc(lg_step, 1)
                    dve.wait_ge(lg_step, i * 4 + 3)
                    nc.vector.tensor_copy(kept.expert[:, i, :], top_i[:, 0:TOPK])
                    dve.wait_ge(s_ex, i + 1)
                    nc.vector.reciprocal(small[:, 5:6], small[:, 5:6]).then_inc(w_step, 1)
                    dve.wait_ge(w_step, i * 2 + 1)
                    nc.vector.tensor_scalar(kept.weights[:, i, :], ex[:, :], small[:, 5:6], kept.gate[:, 1:2],
                                            ALU.mult, ALU.mult).then_inc(w_step, 1)
                    dve.wait_ge(w_step, i * 2 + 2)

                low_of_values(0, 0)
                low_of_values(1, 1)

                def step(i, half, slot, last):
                    add(i)
                    if within(i + 2, TT):
                        low_of_values(i + 2, slot)
                    if within(i - 1, TT):
                        low_of_h(i - 1)
                    close(i, half, slot)
                    if within(i - 2, TT):
                        route(i - 2)
                    if last:
                        route(i - 1)
                        low_of_h(i)
                        route(i)
                in_pairs(dve, TT, step)

            @block.tensor
            def _(pe):
                pe.wait_ge(s_id, 2)

                def transpose_h(i, slot):
                    pe.wait_ge(h_ready, i + 1)
                    after(pe, ht_lo, i)
                    for c in range(KC):
                        done = nc.tensor.transpose(tp[:, c, :], h[:, slot, c * P:(c + 1) * P], ident[:, :])
                    done.then_inc(ht_ready, 1)

                def logits_of(i):
                    pe.wait_ge(ht_lo, i + 1)
                    after(pe, lg_step, i * 4)
                    for c in range(KC):
                        done = three_passes(nc, lg[:, :], [part[:, c, :] for part in ht],
                                            [part[:, c, :] for part in rt], c == 0, c == KC - 1)
                    done.then_inc(lg_ready, 1)

                pe.wait_ge(r_lo, 1)

                def step(i, half, slot, last):
                    pe.wait_ge(ot_lo, i + 1)
                    after(pe, x1_ready, i)
                    for c in range(KC):
                        for n in range(2):
                            cols = slice(n * DM // 2, (n + 1) * DM // 2)
                            done = three_passes(nc, acc[:, cols], [part[:, slot, c, :] for part in ot],
                                                [part[:, c, cols] for part in w], c == 0, c == KC - 1)
                    done.then_inc(acc_ready, 1)
                    if within(i - 1, TT):
                        transpose_h(i - 1, 1 - slot)
                    if within(i - 2, TT):
                        logits_of(i - 2)
                    if last:
                        logits_of(i - 1)
                        transpose_h(i, slot)
                        logits_of(i)
                in_pairs(pe, TT, step)


class Opening:

    PARTS, RING = KC + FC, 4

    def __init__(self, nc, ctx):
        t = Tools(nc, ctx, "opening")
        self.w1 = [t.sb("w1_hi", [P, KC, DM], F32R), t.sb("w1_lo", [P, KC, DM], F32R)]
        self.raw = t.sb("raw", [P, self.RING, DM], F32)
        self.x = t.sb("x", [P, DM], F32)
        self.w_in, self.w_hi, self.w_lo = t.sems("w_in", self.RING), t.sem("w_hi"), t.sem("w_lo")
        self.x_in = t.sem("x_in")


def rank_tokens(nc, kept, h_rows, w1_all, w2_all, opening):
    with ExitStack() as ctx:
        t = Tools(nc, ctx, "r")
        ones = t.sb("ones", [P, P], BF16)
        before = t.sb("before", [P, P], BF16)
        iota_e = t.sb("iota_e", [P, NEXP], F32)
        hot = t.sb("hot", [P, TT, TOPK, NEXP], BF16)
        taken = t.sb("taken", [P, TT, NEXP], BF16)
        sums = t.sb("sums", [P, 2, TT + 1, NEXP], BF16)
        place = t.sb("place", [P, TT, NEXP], F32)
        pick = t.sb("pick", [P, TT, TOPK, NEXP], F32)
        slot_f = t.sb("slot_f", [P, TT, TOPK], F32)
        tile_f = t.sb("tile_f", [P, TT, TOPK], F32)
        tile_i = t.sb("tile_i", [P, TT, TOPK], I32)
        count = t.sb("count", [P, NEXP], F32)
        count_i = t.sb("count_i", [P, NEXP], I32)
        tiles = t.sb("tiles", [P, NEXP], F32)
        ends = t.sb("ends", [P, 2, NEXP], F32)
        first = t.sb("first", [P, NEXP], F32)
        bound_f = t.sb("bound_f", [1, NEXP + 1], F32)
        rank = t.ps("rank", [P, TT, NEXP])
        total = t.ps("total", [P, NEXP])
        s_c, s_v, s_p = t.sem("const"), t.sem("dve"), t.sem("pe")
        sums_at, sums_ready = [], []

        with nc.Block() as block:
            @block.gpsimd
            def _(pool):
                nc.gpsimd.memset(ones[:, :], 1.0).then_inc(s_c, 1)
                nc.gpsimd.iota(iota_e[:, :], pattern=[[1, NEXP]], base=0, channel_multiplier=0,
                               allow_small_or_imprecise_dtypes=True).then_inc(s_c, 1)
                pool.wait_ge(s_c, 2)
                pool.dma_start(opening.x[:, :], h_rows[0:P, :]).then_inc(opening.x_in, 16)
                nc.gpsimd.affine_select(out=before[:, :], in_=ones[:, :], compare_op=ALU.is_gt, fill=0.0, base=0,
                                        pattern=[[1, P]], channel_multiplier=-1).then_inc(s_c, 1)
                for c in range(KC):
                    pool.wait_ge(opening.w_hi, c + 1)
                    nc.gpsimd.tensor_tensor(opening.w1[1][:, c, :], opening.raw[:, c % opening.RING, :],
                                            opening.w1[0][:, c, :].bitcast(F32), ALU.subtract)\
                        .then_inc(opening.w_lo, 1)

            @block.sync
            def _(sp):
                for c in range(opening.PARTS):
                    after(sp, opening.w_lo, c - (opening.RING - 1))
                    src = w1_all[0, c * P:(c + 1) * P, :] if c < KC else w2_all[0, (c - KC) * P:(c - KC + 1) * P, :]
                    sp.dma_start(opening.raw[:, c % opening.RING, :], src).then_inc(opening.w_in[c % opening.RING], 16)

            @block.scalar
            def _(act):
                for c in range(KC):
                    act.wait_ge(opening.w_in[c % opening.RING], 16 * (c // opening.RING) + 16)
                    nc.scalar.copy(opening.w1[0][:, c, :], opening.raw[:, c % opening.RING, :])\
                        .then_inc(opening.w_hi, 1)

            @block.vector
            def _(dve):
                n = [0]

                def link(ins):
                    n[0] += 1
                    ins.then_inc(s_v, 1)
                    dve.wait_ge(s_v, n[0])

                dve.wait_ge(s_c, 3)
                experts = kept.expert[:, :, :].rearrange("p n k -> p (n k)").unsqueeze(2)
                link(nc.vector.tensor_tensor(hot[:, :, :, :].rearrange("p n k e -> p (n k) e"),
                                             experts.to_broadcast([P, TT * TOPK, NEXP]),
                                             iota_e[:, :].unsqueeze(1).to_broadcast([P, TT * TOPK, NEXP]),
                                             ALU.is_equal))
                link(nc.vector.tensor_tensor(taken[:, :, :], hot[:, :, 0, :], hot[:, :, 1, :], ALU.add))
                for k in range(2, TOPK):
                    link(nc.vector.tensor_tensor(taken[:, :, :], taken[:, :, :], hot[:, :, k, :], ALU.add))
                link(nc.vector.memset(sums[:, 0, 0:1, :], 0.0))
                link(nc.vector.memset(sums[:, 1, 0:1, :], 0.0))
                link(nc.vector.tensor_copy(sums[:, 0, 1:TT + 1, :], taken[:, :, :]))
                at, step = 0, 1
                while step < TT + 1:
                    link(nc.vector.tensor_copy(sums[:, 1 - at, 0:step, :], sums[:, at, 0:step, :]))
                    link(nc.vector.tensor_tensor(sums[:, 1 - at, step:TT + 1, :], sums[:, at, step:TT + 1, :],
                                                 sums[:, at, 0:TT + 1 - step, :], ALU.add))
                    at, step = 1 - at, 2 * step
                sums_at.append(at)
                sums_ready.append(n[0])
                dve.wait_ge(s_p, 1)
                link(nc.vector.tensor_scalar(count[:, :], total[:, :], float(P - 1), None, ALU.add))
                link(nc.vector.tensor_copy(count_i[:, :], count[:, :]))
                link(nc.vector.tensor_scalar(count_i[:, :], count_i[:, :], 7, None, ALU.arith_shift_right))
                link(nc.vector.tensor_copy(tiles[:, :], count_i[:, :]))
                link(nc.vector.tensor_scalar(tiles[:, :], tiles[:, :], 2.0, None, ALU.max))
                link(nc.vector.tensor_copy(ends[:, 0, :], tiles[:, :]))
                at, step = 0, 1
                while step < NEXP:
                    link(nc.vector.tensor_copy(ends[:, 1 - at, 0:step], ends[:, at, 0:step]))
                    link(nc.vector.tensor_tensor(ends[:, 1 - at, step:NEXP], ends[:, at, step:NEXP],
                                                 ends[:, at, 0:NEXP - step], ALU.add))
                    at, step = 1 - at, 2 * step
                link(nc.vector.tensor_tensor(first[:, :], ends[:, at, :], tiles[:, :], ALU.subtract))
                link(nc.vector.memset(bound_f[0:1, 0:1], float(TT)))
                link(nc.vector.tensor_scalar(bound_f[0:1, 1:NEXP + 1], ends[0:1, at, :], float(TT), None,
                                             ALU.add))
                link(nc.vector.tensor_copy(kept.bounds[0:1, :], bound_f[0:1, :]))
                link(nc.vector.tensor_scalar(first[:, :], first[:, :], float(P), None, ALU.mult))
                link(nc.vector.tensor_tensor(place[:, :, :], rank[:, :, :],
                                             first[:, :].unsqueeze(1).to_broadcast([P, TT, NEXP]), ALU.add))
                for k in range(TOPK):
                    link(nc.vector.tensor_tensor(pick[:, :, k, :], hot[:, :, k, :], place[:, :, :], ALU.mult))
                link(nc.vector.tensor_reduce(slot_f[:, :, :].rearrange("p n k -> p (n k)"),
                                             pick[:, :, :, :].rearrange("p n k e -> p (n k) e"), AX.X, ALU.add))
                link(nc.vector.tensor_copy(kept.slots[:, :, :], slot_f[:, :, :]))
                link(nc.vector.tensor_scalar(tile_i[:, :, :], kept.slots[:, :, :], 7, None, ALU.arith_shift_right))
                link(nc.vector.tensor_scalar(kept.entries[:, :, :], kept.slots[:, :, :], P - 1, None,
                                             ALU.bitwise_and))
                link(nc.vector.tensor_copy(tile_f[:, :, :], tile_i[:, :, :]))
                link(nc.vector.tensor_copy(slot_f[:, :, :], kept.entries[:, :, :]))
                link(nc.vector.tensor_scalar(slot_f[:, :, :], slot_f[:, :, :], float(MAX_TILES), None, ALU.mult))
                link(nc.vector.tensor_tensor(slot_f[:, :, :], slot_f[:, :, :], tile_f[:, :, :], ALU.add))
                link(nc.vector.tensor_copy(kept.entries[:, :, :], slot_f[:, :, :]))

            @block.tensor
            def _(pe):
                pe.wait_ge(s_c, 3)
                pe.wait_ge(s_v, sums_ready[0])
                done_sums = sums[:, sums_at[0], :, :]
                half = TT // 2
                for u in range(2):
                    out = rank[:, u * half:(u + 1) * half, :]
                    nc.tensor.matmul(out, ones[:, :], done_sums[:, u * half:(u + 1) * half, :], start=True, stop=False)
                    nc.tensor.matmul(out, before[:, :], taken[:, u * half:(u + 1) * half, :], start=False, stop=True)
                nc.tensor.matmul(total[:, :], ones[:, :], done_sums[:, TT, :], start=True, stop=True).then_inc(s_p, 1)


def experts(nc, h_rows, base_rows, y_rows, w1_all, w2_all, table, kept, opening, out):
    with ExitStack() as ctx:
        t_ = Tools(nc, ctx, "e")
        ticks = t_.sem("ticks")
        PARTS, RING = opening.PARTS, opening.RING
        ROUTED_0, LAST = 1, SEGMENTS - 1
        ident = t_.sb("ident", [P, P], F32)
        w1 = [opening.w1, [t_.sb("w1_hi1", [P, KC, DM], F32R), t_.sb("w1_lo1", [P, KC, DM], F32R)]]
        w2 = [t_.sb("w2_hi", [P, FC, DM], F32R), t_.sb("w2_lo", [P, FC, DM], F32R)]
        raw, x = opening.raw, opening.x
        xt = [t_.sb("xt_hi", [P, KC, P], F32R), t_.sb("xt_lo", [P, KC, P], F32R)]
        act_sb = t_.sb("act", [P, FF], F32)
        at = [t_.sb("at_hi", [P, FC, P], F32R), t_.sb("at_lo", [P, FC, P], F32R)]
        y_out = t_.sb("y_out", [P, DM], F32)
        base = t_.sb("base", [P, DM], F32)
        tokens = t_.sb("tokens", [P, MAX_TILES], I32)
        numbers = t_.sb("numbers", [P, TT], I32)
        entry = t_.sb("entry", [P, TOPK], I32)
        number = t_.sb("number", [P, 1], I32)
        index = t_.sb("index", [P, 1], I32)
        free = w1[1 - LAST % 2][0]
        rows = [free[:, k, :].bitcast(F32) for k in range(TOPK)]
        xt_ps = t_.ps("xt_ps", [P, KC, P])
        gu = t_.ps("gu", [P, 2, FF])
        at_ps = t_.ps("at_ps", [P, FC, P])
        y_ps = t_.ps("y_ps", [P, DM])
        hv = h_rows.rearrange("(n p) d -> n p d", p=P)
        bv = base_rows.rearrange("(n p) d -> n p d", p=P)
        yv = y_rows.rearrange("(n p) d -> n p d", p=P)
        outv = out.rearrange("(n p) d -> n p d", p=P)
        s_id = t_.sem("ident")
        w_in, w_hi, w_lo, x_in = opening.w_in, opening.w_hi, opening.w_lo, opening.x_in
        xt_ready, x_hi, x_lo = t_.sem("xt_ready"), t_.sem("x_hi"), t_.sem("x_lo")
        gu_ready, silu_ready, act_ready = t_.sem("gu_ready"), t_.sem("silu_ready"), t_.sem("act_ready")
        at_ready, a_hi, a_lo = t_.sem("at_ready"), t_.sem("a_hi"), t_.sem("a_lo")
        y_ready, y_left, y_right, y_stored = t_.sem("y_ready"), t_.sem("y_left"), t_.sem("y_right"), t_.sem("y_stored")
        base_in = t_.sem("base_in")
        s_table, s_numbers, s_entry, s_scattered = t_.sem("table"), t_.sem("numbers"), t_.sem("entry"), t_.sem("scattered")
        s_index, s_sum = t_.sem("index"), t_.sem("sum")
        s_fill, s_filled = t_.sem("fill"), t_.sem("filled")
        rows_in = t_.sems("rows_in", TOPK)
        HALF = DM // 2

        def segments(eng, step, close_segment):
            def shared(e, kind, kind_before, first):
                step(first, e, e % 2, True, kind, kind_before, 0)
                with eng.Fori(1, TT - 1) as n:
                    step(first + n, e, e % 2, False, kind, kind, n)
                step(first + (TT - 1), e, e % 2, False, kind, kind, TT - 1)
                close_segment(e, e % 2)

            def routed(e, slot, kind_before):
                begin = bound(eng, e - ROUTED_0)
                end = bound(eng, e - ROUTED_0 + 1)
                step(begin, e, slot, True, "routed", kind_before, None)
                with eng.Fori(begin + 1, end) as t:
                    step(t, e, slot, False, "routed", "routed", None)
                close_segment(e, slot)

            shared(0, "shared", None, 0)
            routed(1, 1, "shared")
            routed(2, 0, "routed")
            with eng.Fori(1, NEXP // 2) as j:
                routed(j * 2 + 1, 1, "routed")
                routed(j * 2 + 2, 0, "routed")
            first = bound(eng, NEXP)
            shared(LAST, "last", "routed", first)
            return first

        def bound(eng, j):
            least = TT + 2 * (j if isinstance(j, int) else 2)
            return eng.value_load(kept.bounds[0:1, bass.ds(j, 1)], min_val=least, max_val=TT + MAX_TILES)

        with nc.Block() as block:
            @block.sync
            def _(sp):
                def load(e, chunks):
                    for c in chunks:
                        after(sp, w_lo, e * PARTS + (c - (RING - 1)))
                        carry(sp, ticks)
                        src = w1_all[e, c * P:(c + 1) * P, :] if c < KC else w2_all[e, (c - KC) * P:(c - KC + 1) * P, :]
                        sp.dma_start(raw[:, c % RING, :], src).then_inc(w_in[c % RING], 16)

                load(1, range(KC))
                first_free = bound(sp, NEXP)
                with sp.Fori(0, first_free):
                    sp.sem_inc(s_fill, 16)
                with sp.Fori(first_free, TT + MAX_TILES + 1) as t:
                    sp.wait_ge(s_fill, t * 16)
                    carry(sp, ticks)
                    sp.dma_start(yv[t - TT], hv[0]).then_inc(s_fill, 16)
                sp.wait_ge(s_fill, (TT + MAX_TILES + 1) * 16)
                sp.sem_inc(s_filled, 1)
                load(1, range(KC, PARTS))
                with sp.Fori(2, SEGMENTS) as e:
                    load(e, range(PARTS))

            @block.gpsimd
            def _(pool):
                make_identity(nc, pool, ident, s_id)
                nc.gpsimd.memset(tokens[:, :], 0).then_inc(s_numbers, 1)
                nc.gpsimd.iota(numbers[:, :], pattern=[[P, TT]], base=0, channel_multiplier=1).then_inc(s_numbers, 1)
                pool.wait_ge(s_numbers, 2)
                pool.dma_start(table.rearrange("(p n) o -> p (n o)", p=P), tokens[:, :]).then_inc(s_table, 16)
                pool.wait_ge(s_table, 16)

                def load_x(t, n):
                    after(pool, xt_ready, t * 2)
                    carry(pool, ticks)
                    pool.dma_start(x[:, :], hv[n]).then_inc(x_in, 16)

                def scatter(n):
                    after(pool, s_scattered, n * (16 * TOPK))
                    carry(pool, ticks)
                    nc.gpsimd.tensor_copy(entry[:, :], kept.entries[:, n, :])
                    nc.gpsimd.tensor_copy(number[:, :], numbers[:, bass.ds(n, 1)]).then_inc(s_entry, 1)
                    pool.wait_ge(s_entry, n + 1)
                    carry(pool, ticks)
                    for k in range(TOPK):
                        pool.indirect_dma_start(out=table, out_offset=bass.IndirectOffsetOnAxis(
                            ap=entry[:, k:k + 1], axis=0), in_=number[:, :], in_offset=None)\
                            .then_inc(s_scattered, 16)

                scatter(0)
                with pool.Fori(1, TT) as n:
                    load_x(n, n)
                    scatter(n)
                pool.wait_ge(s_scattered, TT * 16 * TOPK)
                pool.dma_start(tokens[:, :], table.rearrange("(p n) o -> p (n o)", p=P)).then_inc(s_table, 16)
                pool.wait_ge(s_table, 32)

                first = bound(pool, NEXP)
                with pool.Fori(TT, first) as t:
                    pool.wait_ge(xt_ready, t * 2)
                    carry(pool, ticks)
                    nc.gpsimd.tensor_copy(index[:, :], tokens[:, bass.ds(t - TT, 1)]).then_inc(s_index, 1)
                    pool.wait_ge(s_index, t - (TT - 1))
                    carry(pool, ticks)
                    pool.indirect_dma_start(out=x[:, :], out_offset=None, in_=h_rows,
                                            in_offset=bass.IndirectOffsetOnAxis(ap=index[:, :], axis=0))\
                        .then_inc(x_in, 16)

                def gather(n):
                    after(pool, rows_in[TOPK - 1], n * 16)
                    carry(pool, ticks)
                    nc.gpsimd.tensor_copy(entry[:, :], kept.slots[:, n, :]).then_inc(s_entry, 1)
                    pool.wait_ge(s_entry, n + (TT + 1))
                    carry(pool, ticks)
                    for k in range(TOPK):
                        if within(n - 1, TT):
                            pool.wait_ge(s_sum, n * (TOPK + 1) + (k + 2 - (TOPK + 1)))
                            carry(pool, ticks)
                        pool.indirect_dma_start(out=rows[k], out_offset=None, in_=y_rows,
                                                in_offset=bass.IndirectOffsetOnAxis(ap=entry[:, k:k + 1], axis=0))\
                            .then_inc(rows_in[k], 16)

                for n in range(3):
                    load_x(first + n, n)
                pool.wait_ge(y_stored, first * 16 + 16)
                pool.wait_ge(s_filled, 1)
                carry(pool, ticks)
                gather(0)
                with pool.Fori(1, TT - 2) as n:
                    load_x(first + n + 2, n + 2)
                    gather(n)
                gather(TT - 2)
                gather(TT - 1)

            @block.scalar
            def _(act):
                def split(e, slot, c):
                    act.wait_ge(w_in[c % RING], e * (16 * PARTS // RING) + (16 * (c // RING) + 16))
                    dst = w1[slot][0][:, c, :] if c < KC else w2[0][:, c - KC, :]
                    nc.scalar.copy(dst, raw[:, c % RING, :]).then_inc(w_hi, 1)

                def high_of_x(t):
                    for u in range(2):
                        act.wait_ge(xt_ready, t * 2 + (u + 1))
                        cs = slice(u * KC // 2, (u + 1) * KC // 2)
                        nc.scalar.copy(xt[0][:, cs, :], xt_ps[:, cs, :]).then_inc(x_hi, 1)

                act.sem_inc(y_left, 1)
                act.sem_inc(y_stored, 16)

                def left_half(t, kind):
                    act.wait_ge(y_ready, t + 1)
                    act.wait_ge(y_stored, t * 16 + 16)
                    carry(act, ticks)
                    if kind == "routed":
                        nc.scalar.copy(y_out[:, 0:HALF], y_ps[:, 0:HALF]).then_inc(y_left, 1)
                    else:
                        act.sem_inc(y_left, 1)

                def store(t, kind, n):
                    act.wait_ge(y_left, t + 2)
                    act.wait_ge(y_right, t + 2)
                    carry(act, ticks)
                    dst = {"shared": bv, "routed": yv, "last": outv}[kind][t - TT if kind == "routed" else n]
                    act.dma_start(dst, y_out[:, :]).then_inc(y_stored, 16)

                def load_base(n):
                    act.dma_start(base[:, :], bv[n]).then_inc(base_in, 16)

                load_base(0)
                high_of_x(0)

                def step(t, e, slot, fresh, kind, before, n):
                    act.wait_ge(gu_ready, t + 1)
                    nc.scalar.activation(act_sb[:, :], gu[:, 0, :], ACT.Silu).then_inc(silu_ready, 1)
                    if not (kind == "last" and isinstance(n, int) and n == TT - 1):
                        high_of_x(t + 1)
                    if before:
                        left_half(t - 1, before)
                    act.wait_ge(at_ready, t + 1)
                    nc.scalar.copy(at[0][:, :, :], at_ps[:, :, :]).then_inc(a_hi, 1)
                    if before:
                        store(t - 1, before, None if before == "routed" else (TT - 1 if n is None else n - 1))
                        if kind != "routed":
                            load_base(n)
                    if fresh:
                        for c in range(KC, PARTS):
                            split(e, slot, c)
                        if not (isinstance(e, int) and e == LAST):
                            for c in range(KC // 2):
                                split(e + 1, 1 - slot, c)

                def close_segment(e, slot):
                    if not (isinstance(e, int) and e == LAST):
                        for c in range(KC // 2, KC):
                            split(e + 1, 1 - slot, c)

                first = segments(act, step, close_segment)
                left_half(first + (TT - 1), "last")
                store(first + (TT - 1), "last", TT - 1)
                act.wait_ge(y_stored, (first + TT) * 16 + 16)
                carry(act, ticks)

            @block.vector
            def _(dve):
                def split(e, slot, c):
                    dve.wait_ge(w_hi, e * PARTS + (c + 1))
                    w, k = (w1[slot], c) if c < KC else (w2, c - KC)
                    low_part(nc, w[1][:, k, :], raw[:, c % RING, :], w[0][:, k, :]).then_inc(w_lo, 1)

                def low_of_x(t):
                    for u in range(2):
                        dve.wait_ge(x_hi, t * 2 + (u + 1))
                        cs = slice(u * KC // 2, (u + 1) * KC // 2)
                        low_part(nc, xt[1][:, cs, :], xt_ps[:, cs, :], xt[0][:, cs, :]).then_inc(x_lo, 1)

                def finish(t, kind, n):
                    dve.wait_ge(y_ready, t + 1)
                    dve.wait_ge(y_stored, t * 16 + 16)
                    carry(dve, ticks)
                    if kind == "routed":
                        nc.vector.tensor_copy(y_out[:, HALF:DM], y_ps[:, HALF:DM]).then_inc(y_right, 1)
                        return
                    dve.wait_ge(base_in, (n + 1 + (TT if kind == "last" else 0)) * 16)
                    done = nc.vector.scalar_tensor_tensor(y_out[:, :], y_ps[:, :], kept.gate[:, 1:2], base[:, :],
                                                          ALU.mult, ALU.add)
                    if kind == "shared":
                        done.then_inc(y_right, 1)
                        return
                    done.then_inc(s_sum, 1)
                    for k in range(TOPK):
                        dve.wait_ge(s_sum, n * (TOPK + 1) + (k + 1))
                        dve.wait_ge(rows_in[k], (n + 1) * 16)
                        done = nc.vector.scalar_tensor_tensor(y_out[:, :], rows[k], kept.weights[:, n, k:k + 1],
                                                              y_out[:, :], ALU.mult, ALU.add).then_inc(s_sum, 1)
                    dve.wait_ge(s_sum, (n + 1) * (TOPK + 1))
                    dve.sem_inc(y_right, 1)

                dve.sem_inc(y_right, 1)
                low_of_x(0)

                def step(t, e, slot, fresh, kind, before, n):
                    dve.wait_ge(silu_ready, t + 1)
                    nc.vector.tensor_tensor(act_sb[:, :], act_sb[:, :], gu[:, 1, :], ALU.mult).then_inc(act_ready, 1)
                    if not (kind == "last" and isinstance(n, int) and n == TT - 1):
                        low_of_x(t + 1)
                    if before:
                        finish(t - 1, before, None if before == "routed" else (TT - 1 if n is None else n - 1))
                    dve.wait_ge(a_hi, t + 1)
                    low_part(nc, at[1][:, :, :], at_ps[:, :, :], at[0][:, :, :]).then_inc(a_lo, 1)
                    if fresh:
                        for c in range(KC, PARTS):
                            split(e, slot, c)
                        if not (isinstance(e, int) and e == LAST):
                            for c in range(KC // 2):
                                split(e + 1, 1 - slot, c)

                def close_segment(e, slot):
                    if not (isinstance(e, int) and e == LAST):
                        for c in range(KC // 2, KC):
                            split(e + 1, 1 - slot, c)

                first = segments(dve, step, close_segment)
                finish(first + (TT - 1), "last", TT - 1)

            @block.tensor
            def _(pe):
                def transpose_x(t):
                    pe.wait_ge(x_in, t * 16 + 16)
                    after(pe, x_lo, t * 2)
                    for c in range(KC):
                        done = nc.tensor.transpose(xt_ps[:, c, :], x[:, c * P:(c + 1) * P], ident[:, :])
                        if c % (KC // 2) == KC // 2 - 1:
                            done.then_inc(xt_ready, 1)

                def second_product(t):
                    pe.wait_ge(a_lo, t + 1)
                    pe.wait_ge(y_left, t + 1)
                    pe.wait_ge(y_right, t + 1)
                    for c in range(FC):
                        for n in range(2):
                            cols = slice(n * HALF, (n + 1) * HALF)
                            done = three_passes(nc, y_ps[:, cols], [part[:, c, :] for part in at],
                                                [part[:, c, cols] for part in w2], c == 0, c == FC - 1)
                    done.then_inc(y_ready, 1)

                pe.wait_ge(s_id, 2)
                transpose_x(0)

                def step(t, e, slot, fresh, kind, before, n):
                    pe.wait_ge(x_lo, t * 2 + 2)
                    after(pe, act_ready, t)
                    for c in range(KC):
                        if fresh:
                            pe.wait_ge(w_lo, e * PARTS + (c + 1))
                        for u in range(2):
                            done = three_passes(nc, gu[:, u, :], [part[:, c, :] for part in xt],
                                                [part[:, c, u * FF:(u + 1) * FF] for part in w1[slot]],
                                                c == 0, c == KC - 1)
                    done.then_inc(gu_ready, 1)
                    if not (kind == "last" and isinstance(n, int) and n == TT - 1):
                        transpose_x(t + 1)
                    if before:
                        if not fresh:
                            pe.wait_ge(w_lo, e * PARTS + PARTS)
                        second_product(t - 1)
                    pe.wait_ge(act_ready, t + 1)
                    after(pe, a_lo, t)
                    for c in range(FC):
                        done = nc.tensor.transpose(at_ps[:, c, :], act_sb[:, c * P:(c + 1) * P], ident[:, :])
                    done.then_inc(at_ready, 1)

                first = segments(pe, step, lambda e, slot: None)
                second_product(first + (TT - 1))


def program(nc, a, out):
    def scratch(name, shape, dt):
        return nc.dram_tensor(name, shape, dt, kind="Internal").ap()

    q_parts = scratch("q_parts", [BATCH * DM, 2, SEQ], F32)
    k_parts = scratch("k_parts", [BATCH * KV, 2, SEQ], F32)
    v_rows = scratch("v_rows", [BATCH, GROUPS, SEQ, HD], F32)
    o_cols = scratch("o_cols", [BATCH * DM, SEQ], F32)
    with ExitStack() as ctx:
        context = ContextLoads(nc, ctx)
        project_queries(nc, a["x"], a["wq_t"], a["bq_col"], q_parts, context, a["ctx_t"], a["wk_t"], a["wv_t"])
        project_keys(nc, a["ctx_t"], context, a["bk_col"], a["bv"], k_parts, v_rows)
    h_rows = scratch("h_rows", [TOKENS, DM], F32)
    base_rows = scratch("base_rows", [TOKENS, DM], F32)
    with ExitStack() as ctx:
        kept = Kept(nc, ctx)
        with ExitStack() as weights:
            wo = Tools(nc, weights, "wo")
            wo_split = [wo.sb("hi", [P, KC, DM], F32R), wo.sb("lo", [P, KC, DM], F32R)]
            attention(nc, q_parts, k_parts, v_rows, a["mask_s"], a["mask_st"], a["mask_b"], a["mask_b_col"], o_cols,
                      a["wo_t"], wo_split)
            close_attention(nc, a["x"], o_cols, wo_split, a["bo"], a["norm_w"], a["router_t"],
                            (a["g_xattn"], a["g_ffn"]), h_rows, base_rows, kept)
        opening = Opening(nc, ctx)
        rank_tokens(nc, kept, h_rows, a["w1"], a["w2"], opening)
        experts(nc, h_rows, base_rows, scratch("y_rows", [(MAX_TILES + 1) * P, DM], F32), a["w1"], a["w2"],
                scratch("token_table", [P * MAX_TILES, 1], I32), kept, opening, out)


def kernel(x, ctx_2048, mask_SxS2_bc0, mask_BxS2_bk0, g_xattn, g_ffn, L0_xattn_Wq, L0_xattn_bq, L0_xattn_Wk,
           L0_xattn_bk, L0_xattn_Wv, L0_xattn_bv, L0_xattn_Wo, L0_xattn_bo, L0_ffn_norm_w, L0_ffn_router_w,
           L0_ffn_w1, L0_ffn_w2, L0_ffn_sg, L0_ffn_su, L0_ffn_sd):
    import numpy as np
    import concourse.bacc as bacc
    from concourse.bass_utils import run_bass_kernel_spmd

    def c(v):
        return np.ascontiguousarray(v)

    sg, su, sd = (np.asarray(v) for v in (L0_ffn_sg, L0_ffn_su, L0_ffn_sd))

    def segments(shared, routed):
        return np.concatenate([shared(slice(0, FF))[None], routed, shared(slice(FF, 2 * FF))[None]], axis=0)

    mask_s = c(mask_SxS2_bc0)
    mask_b = c(mask_BxS2_bk0)
    arrays = {
        "x": c(x).reshape(TOKENS, DM), "ctx_t": c(np.transpose(np.asarray(ctx_2048), (0, 2, 1))),
        "mask_s": mask_s, "mask_st": c(mask_s.T), "mask_b": mask_b,
        "mask_b_col": c(mask_b.reshape(BATCH, ST, P).transpose(2, 0, 1)),
        "g_xattn": c(g_xattn), "g_ffn": c(g_ffn),
        "wq_t": c(np.asarray(L0_xattn_Wq).T), "bq_col": c(np.asarray(L0_xattn_bq).reshape(KC, P).T),
        "wk_t": c(np.asarray(L0_xattn_Wk).T), "bk_col": c(np.asarray(L0_xattn_bk).reshape(KV // P, P).T),
        "wv_t": c(np.asarray(L0_xattn_Wv).T), "bv": c(L0_xattn_bv),
        "wo_t": c(np.asarray(L0_xattn_Wo).T), "bo": c(L0_xattn_bo),
        "norm_w": c(L0_ffn_norm_w), "router_t": c(np.asarray(L0_ffn_router_w).T),
        "w1": segments(lambda s: np.concatenate([sg[:, s], su[:, s]], axis=1), np.asarray(L0_ffn_w1)),
        "w2": segments(lambda s: sd[s], np.asarray(L0_ffn_w2)),
    }
    nc = bacc.Bacc("TRN2", target_bir_lowering=False, num_devices=1)
    aps = {n: nc.dram_tensor(f"in_{n}", v.shape, U8 if v.dtype == bool else mybir.dt.from_np(v.dtype),
                             kind="ExternalInput").ap()
           for n, v in arrays.items()}
    out = nc.dram_tensor("out", (TOKENS, DM), F32, kind="ExternalOutput").ap()
    program(nc, aps, out)
    r = run_bass_kernel_spmd(nc, [{f"in_{n}": v for n, v in arrays.items()}], core_ids=[0])
    return np.asarray(r.results[0]["out"]).reshape(BATCH, SEQ, DM)
```
